# Optimizing a Trainium2 kernel written in Bass

```python
import numpy as np
import jax
import jax.numpy as jnp

def _softmax(x, axis=-1):
    return jax.nn.softmax(x, axis=axis)

def _gelu(x):
    return jax.nn.gelu(x, approximate=True)

def _silu(x):
    return jax.nn.silu(x)

def _sigmoid(x):
    return jax.nn.sigmoid(x)

def _layernorm(x, axis=-1, eps=1e-05):
    m = jnp.mean(x, axis=axis, keepdims=True)
    v = jnp.var(x, axis=axis, keepdims=True)
    return (x - m) / jnp.sqrt(v + eps)

def _scatter_add(tgt, idx, src, axis=0):
    return tgt.at[idx].add(src)

def _segment_sum(src, seg, n):
    return jax.ops.segment_sum(src, seg, n)
kernel_name = 'mk_decoder_postln_d1_seqx_r4_fd9e85'

def setup_inputs(seed: int=0):
    np.random.seed(seed)
    _w = jnp.asarray

    def _rec_inputs():
        import jax
        import jax.numpy as jnp
        _rk = jax.random.key(seed)
        x = 7.22e-05 + 1 * jax.random.normal(jax.random.fold_in(_rk, 1), (32, 256, 256), jnp.float32)
        _lenS = 256 - jax.random.randint(jax.random.fold_in(_rk, 7), (32,), 0, max(1, 256 // 4) + 1, jnp.int32)
        _lenS2 = 77 - jax.random.randint(jax.random.fold_in(_rk, 8), (32,), 0, max(1, 77 // 4) + 1, jnp.int32)
        _ctx_1024P = jax.random.normal(jax.random.fold_in(_rk, 11), (32, 16, 256), jnp.float32)
        _ctx_1024c = jax.random.dirichlet(jax.random.fold_in(_rk, 511), 0.3 * jnp.ones((16,), jnp.float32), (32, 77))
        _ctx_1024t = jnp.einsum('bsk,bkd->bsd', _ctx_1024c, _ctx_1024P)
        _ctx_1024t = _ctx_1024t * jax.lax.rsqrt(jnp.mean(jnp.square(_ctx_1024t)) + 1e-12) * 0.953939
        ctx_1024 = -1.81876e-05 + 0.999925 * (_ctx_1024t + 0.3 * jax.random.normal(jax.random.fold_in(_rk, 611), (32, 77, 256), jnp.float32))
        _validS = jnp.arange(256)[None, :] < _lenS[:, None]
        _validS2 = jnp.arange(77)[None, :] < _lenS2[:, None]
        _causal = jnp.tril(jnp.ones((256, 256), dtype=bool))
        mask_BxS2xS_ik0 = jnp.where(jnp.broadcast_to(_validS[:, None, :], (32, 77, 256)), 0, 1).astype(jnp.int32)
        return (x, ctx_1024, mask_BxS2xS_ik0)
    x, ctx_1024, mask_BxS2xS_ik0 = _rec_inputs()

    def _L0_attn_setup():
        import jax, jax.numpy as jnp
        import numpy as np
        D_MODEL = 256
        N_HEADS = 16
        D_HEAD = 64
        GROUP_SIZE = 2
        N_GROUPS = N_HEADS // GROUP_SIZE
        key = jax.random.key(seed)
        k1, k2, k3, k4, k5 = jax.random.split(key, 5)

        def xavier(k, shape):
            fan_in, fan_out = (shape[0], int(np.prod(shape[1:])))
            bound = float(np.sqrt(6.0 / (fan_in + fan_out)))
            return jax.random.uniform(k, shape, jnp.float32, -bound, bound)
        return {'resid': jax.random.normal(k1, (2, 512, D_MODEL), jnp.float32), 'W_Q': xavier(k2, (D_MODEL, N_HEADS, D_HEAD)), 'W_K': xavier(k3, (D_MODEL, N_GROUPS, D_HEAD)), 'W_V': xavier(k4, (D_MODEL, N_GROUPS, D_HEAD)), 'W_out': xavier(k5, (D_HEAD, N_HEADS, D_MODEL)), 'b_out': jnp.zeros((D_MODEL,), jnp.float32)}
    _L0_attn_all = _L0_attn_setup()
    _L0_attn_in = {k: v for k, v in _L0_attn_all.items() if k in ('W_Q', 'W_K', 'W_V', 'W_out', 'b_out')}
    del _L0_attn_all

    def _L0_xattn_setup():
        import jax, jax.numpy as jnp
        import numpy as np
        B, T, V, C = (32, 64, 250, 256)
        H, DH = (8, 64)
        INNER = H * DH
        K = 5
        SCALE = DH ** (-0.5)

        def layer_norm(x, w, b, eps=1e-05):
            mu = jnp.mean(x, axis=-1, keepdims=True)
            var = jnp.mean(jnp.square(x - mu), axis=-1, keepdims=True)
            return (x - mu) * jax.lax.rsqrt(var + eps) * w + b
        key = jax.random.key(seed)
        ks = jax.random.split(key, 8)
        x = jax.random.normal(ks[0], (B, T, C), dtype=jnp.float32)
        vision = jax.random.normal(ks[1], (B, V, C), dtype=jnp.float32)
        idx = jax.random.randint(ks[2], (B, T, K), 0, V)
        mask = jnp.zeros((B, V, T), jnp.int32)
        mask = mask.at[jnp.arange(B)[:, None, None], idx, jnp.arange(T)[None, :, None]].set(1)
        Wq = jax.random.normal(ks[3], (C, INNER), dtype=jnp.float32) * 0.02
        Wkv = jax.random.normal(ks[4], (C, 2 * INNER), dtype=jnp.float32) * 0.02
        Wout = jax.random.normal(ks[5], (INNER, C), dtype=jnp.float32) * 0.02
        return {'x': x, 'vision': vision, 'ln_w': jnp.ones((C,), jnp.float32), 'ln_b': jnp.zeros((C,), jnp.float32), 'Wq': Wq, 'Wkv': Wkv, 'Wout': Wout, 'attention_mask': mask, 'num_support': K}
    _L0_xattn_all = _L0_xattn_setup()
    _L0_xattn_in = {k: v for k, v in _L0_xattn_all.items() if k in ('ln_w', 'ln_b', 'Wq', 'Wkv', 'Wout')}
    del _L0_xattn_all

    def _L0_ffn_setup():
        import jax, jax.numpy as jnp
        import numpy as np
        DIM = 256
        HIDDEN = 768
        SCALE = 1.0 / 127.0

        def _dequant(w_int, dtype):
            return w_int.astype(dtype) * jnp.asarray(SCALE, dtype)
        key = jax.random.key(seed)
        k_x, k_g, k_u, k_d = jax.random.split(key, 4)
        x = jax.random.normal(k_x, (4, 512, DIM), dtype=jnp.float32)
        w_gate = jax.random.randint(k_g, (HIDDEN, DIM), -127, 128, dtype=jnp.int32)
        w_up = jax.random.randint(k_u, (HIDDEN, DIM), -127, 128, dtype=jnp.int32)
        w_down = jax.random.randint(k_d, (DIM, HIDDEN), -127, 128, dtype=jnp.int32)
        return {'x': x, 'w_gate': w_gate, 'w_up': w_up, 'w_down': w_down}
    _L0_ffn_all = _L0_ffn_setup()
    _L0_ffn_in = {k: v for k, v in _L0_ffn_all.items() if k in ('w_gate', 'w_up', 'w_down')}
    del _L0_ffn_all
    return {'x': x, 'ctx_1024': ctx_1024, 'mask_BxS2xS_ik0': mask_BxS2xS_ik0, 'L0_attn_W_Q': _L0_attn_in['W_Q'], 'L0_attn_W_K': _L0_attn_in['W_K'], 'L0_attn_W_V': _L0_attn_in['W_V'], 'L0_attn_W_out': _L0_attn_in['W_out'], 'L0_attn_b_out': _L0_attn_in['b_out'], 'L0_xattn_ln_w': _L0_xattn_in['ln_w'], 'L0_xattn_ln_b': _L0_xattn_in['ln_b'], 'L0_xattn_Wq': _L0_xattn_in['Wq'], 'L0_xattn_Wkv': _L0_xattn_in['Wkv'], 'L0_xattn_Wout': _L0_xattn_in['Wout'], 'L0_ffn_w_gate': _L0_ffn_in['w_gate'], 'L0_ffn_w_up': _L0_ffn_in['w_up'], 'L0_ffn_w_down': _L0_ffn_in['w_down']}

def reference(x, ctx_1024, mask_BxS2xS_ik0, L0_attn_W_Q, L0_attn_W_K, L0_attn_W_V, L0_attn_W_out, L0_attn_b_out, L0_xattn_ln_w, L0_xattn_ln_b, L0_xattn_Wq, L0_xattn_Wkv, L0_xattn_Wout, L0_ffn_w_gate, L0_ffn_w_up, L0_ffn_w_down):
    import jax
    import jax.numpy as jnp

    def _L0_attn_ref(resid, W_Q, W_K, W_V, W_out, b_out):
        import jax, jax.numpy as jnp
        import numpy as np
        D_MODEL = 256
        N_HEADS = 16
        D_HEAD = 64
        GROUP_SIZE = 2
        N_GROUPS = N_HEADS // GROUP_SIZE
        batch, seq, _ = resid.shape
        q = jnp.einsum('bsd,dhe->bshe', resid, W_Q)
        q = q.reshape(batch, seq, N_GROUPS, GROUP_SIZE, D_HEAD)
        k = jnp.einsum('bsd,dge->bsge', resid, W_K)
        v = jnp.einsum('bsd,dge->bsge', resid, W_V)
        scores = jnp.einsum('bqgre,bkge->bgrqk', q, k) / jnp.sqrt(jnp.float32(D_HEAD))
        causal_mask = jnp.triu(jnp.ones((seq, seq), bool), k=1)
        scores = jnp.where(causal_mask, jnp.float32(-1000000.0), scores)
        probs = jax.nn.softmax(scores, axis=-1)
        z = jnp.einsum('bgrqk,bkge->bqgre', probs, v)
        z = z.reshape(batch, seq, N_HEADS, D_HEAD)
        out = jnp.einsum('bshe,ehd->bsd', z, W_out) + b_out
        return out

    def _L0_xattn_ref(x, vision, ln_w, ln_b, Wq, Wkv, Wout, attention_mask, num_support):
        import jax, jax.numpy as jnp
        import numpy as np
        B, T, V, C = (32, 64, 250, 256)
        H, DH = (8, 64)
        INNER = H * DH
        K = 5
        SCALE = DH ** (-0.5)

        def layer_norm(x, w, b, eps=1e-05):
            mu = jnp.mean(x, axis=-1, keepdims=True)
            var = jnp.mean(jnp.square(x - mu), axis=-1, keepdims=True)
            return (x - mu) * jax.lax.rsqrt(var + eps) * w + b
        Bb, Tt, Cc = x.shape
        Vv = vision.shape[1]
        am_t = jnp.transpose(attention_mask, (0, 2, 1))
        idxs = jnp.where(am_t != 0, jnp.arange(Vv, dtype=jnp.int32), Vv)
        padded = -jax.lax.top_k(-idxs, num_support)[0]
        vision_pad = jnp.concatenate([vision, jnp.zeros((Bb, 1, Cc), vision.dtype)], axis=1)
        vg = vision_pad[jnp.arange(Bb)[:, None, None], padded]
        valid = padded != Vv
        xn = layer_norm(x, ln_w, ln_b)
        q = jnp.einsum('btc,ce->bte', xn, Wq) * SCALE
        kv = jnp.einsum('btkc,ce->btke', vg, Wkv)
        k, v = jnp.split(kv, 2, axis=-1)
        qh = q.reshape(Bb, Tt, H, DH)
        kh = k.reshape(Bb, Tt, num_support, H, DH)
        vh = v.reshape(Bb, Tt, num_support, H, DH)
        sim = jnp.einsum('bthd,btkhd->bthk', qh, kh)
        sim = sim + jnp.where(valid, 0.0, -10000.0)[:, :, None, :]
        attn = jax.nn.softmax(sim, axis=-1)
        attn = attn * valid[:, :, None, :].astype(attn.dtype)
        out = jnp.einsum('bthk,btkhd->bthd', attn, vh).reshape(Bb, Tt, INNER)
        return jnp.einsum('bte,ec->btc', out, Wout)

    def _L0_ffn_ref(x, w_gate, w_up, w_down):
        import jax, jax.numpy as jnp
        import numpy as np
        DIM = 256
        HIDDEN = 768
        SCALE = 1.0 / 127.0

        def _dequant(w_int, dtype):
            return w_int.astype(dtype) * jnp.asarray(SCALE, dtype)
        wg = _dequant(w_gate, x.dtype)
        wu = _dequant(w_up, x.dtype)
        wd = _dequant(w_down, x.dtype)
        gate = jnp.einsum('bsd,hd->bsh', x, wg)
        up = jnp.einsum('bsd,hd->bsh', x, wu)
        h = jax.nn.silu(gate) * up
        return jnp.einsum('bsh,dh->bsd', h, wd)
    x = _layernorm(x + _L0_attn_ref(x, L0_attn_W_Q, L0_attn_W_K, L0_attn_W_V, L0_attn_W_out, L0_attn_b_out), axis=-1)
    x = _layernorm(x + _L0_xattn_ref(x, ctx_1024, L0_xattn_ln_w, L0_xattn_ln_b, L0_xattn_Wq, L0_xattn_Wkv, L0_xattn_Wout, mask_BxS2xS_ik0, 5), axis=-1)
    x = _layernorm(x + _L0_ffn_ref(x, L0_ffn_w_gate, L0_ffn_w_up, L0_ffn_w_down), axis=-1)
    return x

_drawn_inputs = setup_inputs


def setup_inputs(seed=0):
    import zlib

    import numpy as np

    out = dict(_drawn_inputs(seed))
    spreads = {'L0_attn_b_out': (0.0, 0.1), 'L0_xattn_ln_w': (1.0, 0.6), 'L0_xattn_ln_b': (0.0, 2.0)}
    factors = {'L0_xattn_Wq': 8.0}
    for name, (base, spread) in spreads.items():
        noise = np.random.default_rng([zlib.crc32(name.encode()), seed]).standard_normal(out[name].shape)
        drawn = base * np.exp(spread * noise) if base else spread * noise
        out[name] = jnp.asarray(drawn.astype(out[name].dtype))
    for name, factor in factors.items():
        out[name] = (out[name] * factor).astype(out[name].dtype)
    return out
```

```python
from contextlib import ExitStack

import concourse.bass as bass
from concourse import mybir

F32 = mybir.dt.float32
F32R = mybir.dt.float32r
I32 = mybir.dt.int32
ALU = mybir.AluOpType
ACT = mybir.ActivationFunctionType
AX_X = mybir.AxisListType.X

P = 128
EPS = 1e-5
NEG = -1e30
PAD_BIAS = -10000.0
TOP = 5
QUANT = 1.0 / 127.0


class Signal:

    def __init__(self, nc, ctx, name, per_batch, unit=1):
        self.sem = ctx.enter_context(nc.semaphore(name))
        self.per_batch = per_batch
        self.unit = unit

    def at(self, batch, count):
        value = (batch * self.per_batch + count) * self.unit
        return max(value, 0) if isinstance(value, int) else value


class Chain:

    def __init__(self, nc, ctx, name, per_batch):
        self.sem = ctx.enter_context(nc.semaphore(name))
        self.per_batch = per_batch
        self.n = 0

    def begin(self):
        self.n = 0

    def next(self):
        self.n += 1
        return self.sem

    def so_far(self, batch):
        return batch * self.per_batch + self.n

    def end(self):
        assert self.n == self.per_batch, (self.n, self.per_batch)


STEPS = 10
BEFORE = ["aQ0", "aK0", "aV0", "aV1"]
FILL = [
    ["rT10", "rT11", "rXK", "rXV", "aQ1"],
    ["rXQ0", "rXQ1"],
    ["rSIM00", "rSIM01", "aQ2", "aK1"],
    ["rSIM10", "rSIM11"],
    ["rT200", "rT201", "aQ3"],
    ["rXPV0", "rT210", "rT211"],
    ["rXPV1", "rXOUT"],
    ["rT30", "rT31", "rFFN0", "rFFN1", "rFFN2"],
    ["rDOWN0", "rFFN3", "rFFN4"],
    ["rFFN5", "rDOWN1"],
]
AFTER = ["aOUT"]
BANKS = 3


class Phase:

    def __init__(self, b, attn, rest, turn):
        self.b, self.rb, self.attn, self.rest, self.turn = b, b - 1, attn, rest, turn
        names = BEFORE + [n for step in FILL for n in step] + AFTER
        self.names = [n for n in names if (attn and n[0] == "a") or (rest and n[0] == "r")]
        assert len(self.names) % BANKS == 0
        self.index = {n: i for i, n in enumerate(self.names)}

    def fillers(self, step):
        return [n for n in FILL[step] if n in self.index]

    def bank(self, name):
        return self.index[name] % BANKS

    def full(self, name):
        return self.turn * BANKS + self.index[name] + 1

    def read(self, *names, before=None):
        counts = {}
        for name in names + (before,) * (before is not None):
            turns = self.index[name] // BANKS + (name != before)
            counts[self.bank(name)] = max(turns, counts.get(self.bank(name), 0))
        return [(bank, self.turn + turns) for bank, turns in counts.items()]


def decoder_layer(nc, x, xT, ctxT, maskT, wq, wk, wv, wo, b_out, ln_w, ln_b, xwq, xwkv, xwo, wg, wu, wd, out):
    B, S, D = x.shape
    V = ctxT.shape[2]
    KD = D // P
    T = S // P
    HE = wq.shape[1]
    KE = wk.shape[1]
    E = 64
    NP = HE // P
    NJ = KE // P
    XE = xwq.shape[1]
    XP = XE // P
    XH = XE // E
    HID = wg.shape[1]
    KH = HID // P
    SCALE = E ** -0.5
    PAIR = T * S + T * P

    PASSES = B - 1
    USES_A = sum(n[0] == "a" for n in BEFORE + sum(FILL, []) + AFTER)
    USES_R = sum(n[0] == "r" for n in sum(FILL, []))
    TURN_A, TURN_ALL = USES_A // BANKS, (USES_A + USES_R) // BANKS

    def phases(eng, body):
        body(Phase(0, True, False, 0))
        with eng.Fori(1, B) as b:
            body(Phase(b, True, True, b * TURN_ALL + (TURN_A - TURN_ALL)))
        body(Phase(B, False, True, TURN_A + PASSES * TURN_ALL))

    with ExitStack() as ctx:
        def sb(name, shape, dt=F32):
            return ctx.enter_context(nc.sbuf_tensor(name, shape, dt))

        def signal(name, per_batch, unit=1):
            return Signal(nc, ctx, name, per_batch, unit)

        def halves(name, shape):
            return sb(name + "_hi", shape, F32R), sb(name + "_lo", shape, F32R)

        wq_s = halves("wq", [P, KD, HE])
        wk_s = halves("wk", [P, KD, KE])
        wv_s = halves("wv", [P, KD, KE])
        wo_s = halves("wo", [P, NP, D])
        xwq_s = halves("xwq", [P, KD, XE])
        xwk = sb("xwk", [P, KD, XE])
        xwv_s = halves("xwv", [P, KD, XE])
        xwo_s = halves("xwo", [P, XP, D])
        wg_s = halves("wg", [P, KD, HID])
        wu_s = halves("wu", [P, KD, HID])
        wd_s = halves("wd", [P, KH, D])
        lnw = sb("lnw", [P, KD])
        lnb = sb("lnb", [P, KD])
        bias = sb("bias", [P, D])
        ident = sb("ident", [P, P])
        causal = sb("causal", [P, S])
        ones = sb("ones", [P, V])
        minus_half = sb("minus_half", [P, T])
        eps = sb("eps", [P, T])

        x_in = sb("x_in", [P, T, D])
        xT_in = sb("xT_in", [P, KD, S])
        xT_s = halves("xTs", [P, KD, S])
        QT = sb("QT", [P, 2, 2, S])
        KB = sb("KB", [P, NJ, 2, S])
        Vt = sb("Vt", [P, T, KE])
        SM = sb("SM", [P, 2, PAIR])
        least = sb("least", [P, 2, 4])
        total = sb("total", [P, 2, 4])
        PT = sb("PT", [P, 2, PAIR])
        Z_s = halves("Z", [P, NP, S])

        X = sb("X", [P, T, D])
        XN = sb("XN", [P, T * D])
        XN_t = XN[:, :].rearrange("p (t d) -> p t d", t=T)
        NT_s = halves("NT", [P, KD, S])
        stats = sb("stats", [P, T, 6])
        moments = sb("moments", [P, T, 2])
        var = sb("var", [P, T])
        rstd = sb("rstd", [P, T])
        ctx_in = sb("ctx_in", [P, KD, P])
        ctx_s = halves("ctxs", [P, KD, P])
        mask_in = sb("mask_in", [P, T, V], I32)
        allowed = sb("allowed", [P, T, V])
        taken = sb("taken", [P, T, V])
        count = sb("count", [P, T, 2])
        pad_bias = sb("pad_bias", [P, T])
        KX = sb("KX", [P, XP, 2 * V])
        VX = sb("VX", [P, XE])
        SX = sb("SX", [P, XH, V])
        PX = sb("PX", [P, XH, P])
        pmax = sb("pmax", [P, 3, XH])
        den = sb("den", [P, 2, XH])
        QX = sb("QX", [P, XH * P])
        QX_q = QX[:, :].rearrange("p (c s) -> p c s", c=XP)
        QX_p = QX[:, :].rearrange("p (h s) -> p h s", h=XH)
        G = sb("G", [P, 2, S])
        H_s = halves("H", [P, KH // 2, S])
        ZX_s = [z[:, NP - XP:NP, :] for z in Z_s]

        stage = [PX[:, :, :].rearrange("p h s -> p (h s)"), QX[:, :]]

        def bank(name):
            return ctx.enter_context(nc.psum_tensor(name, [P, 512], F32))

        gen = [bank(f"gen{i}") for i in range(BANKS)]
        s_ps = [bank(f"s_ps{i}") for i in range(2)]
        pt_ps = [bank(f"pt_ps{i}") for i in range(2)]
        z_ps = bank("z_ps")

        staged = [signal(f"staged{i}", 0, 16) for i in range(2)]
        w_high = signal("w_high", 0)
        w_low = signal("w_low", 0)
        small_in = signal("small_in", 0, 16)
        pool_set = signal("pool_set", 0)
        xT_loaded = signal("xT_loaded", 1, 16)
        x_loaded = signal("x_loaded", 1, 16)
        ctx_loaded = signal("ctx_loaded", 1, 16)
        mask_loaded = signal("mask_loaded", 1, 16)
        out_stored = signal("out_stored", 1, 16)
        gen_full = ctx.enter_context(nc.semaphore("gen_full"))
        gen_read = [ctx.enter_context(nc.semaphore(f"gen_read{i}")) for i in range(BANKS)]
        xT_high = signal("xT_high", 1)
        xT_low = signal("xT_low", 1)
        x_biased = signal("x_biased", 1)
        s_full = signal("s_full", 2 * NP)
        s_masked = signal("s_masked", 2 * NP)
        exp_done = signal("exp_done", NP)
        p_ready = signal("p_ready", NP)
        pt_full = signal("pt_full", 2 * NP)
        pt0_ready = signal("pt0_ready", NP)
        pt1_ready = signal("pt1_ready", NP)
        z_full = signal("z_full", NP)
        z_high = signal("z_high", NP // 2)
        z_low = signal("z_low", NP // 2)
        xn_ready = signal("xn_ready", 1)
        moments_a = signal("moments_a", 2)
        rstd_a = signal("rstd_a", 2)
        dve_a = Chain(nc, ctx, "dve_a", NP + 3)
        pool_a = Chain(nc, ctx, "pool_a", 2)
        moments_r = signal("moments_r", 2)
        rstd_r = signal("rstd_r", 2)
        nt_high = signal("nt_high", 3)
        nt_low = signal("nt_low", 1)
        ctx_high = signal("ctx_high", 1)
        ctx_low = signal("ctx_low", 1)
        mask_read = signal("mask_read", 1)
        sx_shifted = signal("sx_shifted", 2)
        sx_exp = signal("sx_exp", 2)
        px_ready = signal("px_ready", 2)
        zx_high = signal("zx_high", 2)
        x2_ready = signal("x2_ready", 1)
        tanh_done = signal("tanh_done", KH)
        h_high = signal("h_high", KH)
        h_low = signal("h_low", KH)
        out_ready = signal("out_ready", 1)
        waited = ctx.enter_context(nc.semaphore("waited"))
        dve_r = Chain(nc, ctx, "dve_r", 22)
        pool_r = Chain(nc, ctx, "pool_r", 2)

        weights = []
        for w, parts, per in ((wq, wq_s, 1), (wk, wk_s, 2), (wv, wv_s, 2), (wo, wo_s, 4), (xwkv[:, XE:], xwv_s, 2),
                              (xwq, xwq_s, 2), (xwo, xwo_s, 4), (wg, wg_s, 1), (wu, wu_s, 1), (wd, wd_s, 3)):
            rows = w.rearrange("(k p) n -> p k n", p=P)
            for k in range(0, rows.shape[1], per):
                weights.append((rows[:, k:k + per, :], [part[:, k:k + per, :] for part in parts], per, rows.shape[2]))

        def stage_of(n):
            _, _, per, cols = weights[n]
            flat = stage[n % 2][:, 0:per * cols].rearrange("p (k n) -> p k n", k=per)
            return flat if weights[n][0].dtype == F32 else flat.bitcast(I32)

        EARLY = 4
        late_weights = [[] for _ in range(STEPS)]
        for n in range(EARLY, len(weights)):
            late_weights[(n - EARLY) * STEPS // (len(weights) - EARLY)].append(n)
        SETS = 10

        def halves_view(t):
            return t.rearrange("p (c s) -> p c s", c=2)

        block = ctx.enter_context(nc.Block())

        @block.sync
        def _(sp):
            def load_xT(b):
                sp.wait_ge(xT_high.sem, xT_high.at(b, 0))
                sp.wait_ge(xT_low.sem, xT_low.at(b, 0))
                sp.dma_start(xT_in[:, :, :], xT[b].rearrange("(k p) s -> p k s", p=P)).then_inc(xT_loaded.sem, 16)

            def load_x(b):
                sp.wait_ge(moments_a.sem, moments_a.at(b, -1))
                sp.dma_start(x_in[:, :, :], x[b].rearrange("(t p) d -> p t d", p=P)).then_inc(x_loaded.sem, 16)

            def load_ctx(b):
                if not isinstance(b, int) or b > 0:
                    sp.wait_ge(s_full.sem, s_full.at(b, 3))
                sp.dma_start(ctx_in[:, :, 0:V], ctxT[b].rearrange("(k p) v -> p k v", p=P)).then_inc(ctx_loaded.sem, 16)
                sp.wait_ge(mask_read.sem, mask_read.at(b, 0))
                sp.dma_start(mask_in[:, :, :], maskT[b].rearrange("(t p) v -> p t v", p=P)).then_inc(mask_loaded.sem, 16)

            def store(b):
                sp.wait_ge(out_ready.sem, out_ready.at(b, 1))
                sp.dma_start(out[b].rearrange("(t p) d -> p t d", p=P), XN_t).then_inc(out_stored.sem, 16)

            load_xT(0)
            for n in range(len(weights)):
                if n >= 2:
                    sp.wait_ge(w_low.sem, w_low.at(0, n - 1))
                sp.dma_start(stage_of(n), weights[n][0]).then_inc(staged[n % 2].sem, 16)
                if n == 1:
                    sp.dma_start(bias[:, :], b_out.partition_broadcast(P)).then_inc(small_in.sem, 16)
                    sp.dma_start(lnw[:, :], ln_w).then_inc(small_in.sem, 16)
                    sp.dma_start(lnb[:, :], ln_b).then_inc(small_in.sem, 16)
                    sp.dma_start(xwk[:, :, :], xwkv[:, 0:XE].rearrange("(k p) n -> p k n", p=P)).then_inc(small_in.sem, 16)
                    load_x(0)
                if n == 3:
                    sp.wait_ge(pool_set.sem, pool_set.at(0, SETS))
                    load_ctx(0)
            load_xT(1)
            load_x(1)
            with sp.Fori(1, B - 1) as b:
                load_ctx(b)
                load_xT(b + 1)
                store(b - 1)
                load_x(b + 1)
            load_ctx(B - 1)
            store(B - 2)
            store(B - 1)
            sp.wait_ge(out_stored.sem, out_stored.at(B - 1, 1))

        @block.tensor
        def _(pe):
            def split_product(o, left, right, first=True, last=True):
                pe.matmul(o, left[0], right[0], start=first, stop=False)
                pe.matmul(o, left[0], right[1], start=False, stop=False)
                return pe.matmul(o, left[1], right[0], start=False, stop=last)

            def project(o, left, right, k_tiles):
                for k in range(k_tiles):
                    ins = split_product(o, left(k), right(k), k == 0, k == k_tiles - 1)
                return ins

            def tile_of(parts, cols):
                return lambda k: [part[:, k, cols] for part in parts]

            def body(ph):
                b, rb = ph.b, ph.rb
                whole = slice(None)

                def inputs_of(name):
                    kind, last = name[1:], name[-1]
                    if kind[:3] == "SIM":
                        return f"rXQ{last}", "rXK"
                    if kind[:3] == "XPV":
                        return "rXV", f"rT2{last}0", f"rT2{last}1"
                    if kind == "XOUT":
                        return "rXPV0", "rXPV1"
                    if kind[:3] == "FFN":
                        return "rT30", "rT31"
                    return ()

                def fill(name):
                    for bank, value in ph.read(*inputs_of(name), before=name):
                        pe.wait_ge(gen_read[bank], value)
                    ps = gen[ph.bank(name)]
                    two = halves_view(ps[:, :])
                    kind, c = name[1:], int(name[-1]) if name[-1].isdigit() else 0
                    if kind[0] in "QK":
                        parts = wq_s if kind[0] == "Q" else wk_s
                        for i in range(2):
                            m = slice((2 * c + i) * P, (2 * c + i + 1) * P)
                            ins = project(two[:, i, :], tile_of(parts, m), tile_of(xT_s, whole), KD)
                    elif kind[0] == "V":
                        ins = project(ps[:, :], tile_of(xT_s, slice(c * P, (c + 1) * P)), tile_of(wv_s, whole), KD)
                    elif kind == "OUT":
                        pe.wait_ge(z_low.sem, z_low.at(b, NP // 2))
                        for t in range(T):
                            ins = project(two[:, t, :], tile_of(Z_s, slice(t * P, (t + 1) * P)),
                                          tile_of(wo_s, whole), NP)
                    elif kind[:2] == "T1":
                        pe.wait_ge(xn_ready.sem, xn_ready.at(rb, 1))
                        for t in range(T):
                            ins = pe.transpose(ps[:, t * P:(t + 1) * P], XN_t[:, t, c * P:(c + 1) * P], ident[:, :])
                    elif kind == "XK":
                        pe.wait_ge(ctx_loaded.sem, ctx_loaded.at(rb, 1))
                        for m in range(XP):
                            for k in range(KD):
                                ins = pe.matmul(ps[:, m * P:(m + 1) * P], xwk[:, k, m * P:(m + 1) * P],
                                                ctx_in[:, k, :], start=(k == 0), stop=(k == KD - 1))
                    elif kind == "XV":
                        pe.wait_ge(ctx_low.sem, ctx_low.at(rb, 1))
                        ins = project(ps[:, :], tile_of(ctx_s, whole), tile_of(xwv_s, whole), KD)
                    elif kind[:2] == "XQ":
                        pe.wait_ge(nt_low.sem, nt_low.at(rb, 1))
                        for i in range(2):
                            m = slice((2 * c + i) * P, (2 * c + i + 1) * P)
                            ins = project(two[:, i, :], tile_of(xwq_s, m), tile_of(NT_s, whole), KD)
                    elif kind[:3] == "SIM":
                        t = int(kind[3])
                        for i in range(2):
                            p = 2 * c + i
                            ins = pe.matmul(ps[:, i * 2 * V:(i + 1) * 2 * V], QX_q[:, p, t * P:(t + 1) * P],
                                            KX[:, p, :], start=True, stop=True)
                    elif kind[:2] == "T2":
                        t = int(kind[2])
                        pe.wait_ge(px_ready.sem, px_ready.at(rb, t + 1))
                        for i in range(4):
                            ins = pe.transpose(ps[:, i * P:(i + 1) * P], PX[:, 4 * c + i, :], ident[:, :])
                    elif kind[:3] == "XPV":
                        for h in range(XH):
                            ins = pe.matmul(ps[E * (h % 2):E * (h % 2 + 1), h // 2 * P:(h // 2 + 1) * P],
                                            VX[:, h * E:(h + 1) * E], QX_p[:, h, :], start=True, stop=True)
                    elif kind == "XOUT":
                        for t in range(T):
                            ins = project(two[:, t, :], tile_of(ZX_s, slice(t * P, (t + 1) * P)),
                                          tile_of(xwo_s, whole), XP)
                    elif kind[:2] == "T3":
                        pe.wait_ge(x2_ready.sem, x2_ready.at(rb, 1))
                        for t in range(T):
                            ins = pe.transpose(ps[:, t * P:(t + 1) * P], X[:, t, c * P:(c + 1) * P], ident[:, :])
                    elif kind[:3] == "FFN":
                        for i, parts in enumerate((wg_s, wu_s)):
                            ins = project(two[:, i, :], tile_of(parts, slice(c * P, (c + 1) * P)),
                                          tile_of(NT_s, whole), KD)
                    elif kind[:4] == "DOWN":
                        half = KH // 2
                        pe.wait_ge(h_low.sem, h_low.at(rb, half * (c + 1)))
                        for t in range(T):
                            ins = project(two[:, t, :], tile_of(H_s, slice(t * P, (t + 1) * P)),
                                          lambda k: [w[:, half * c + k, :] for w in wd_s], half)
                    ins.then_inc(gen_full, 1)

                def scores(i):
                    q = QT[:, i // 2 % 2, i % 2, :]
                    for bank, value in ph.read(f"aQ{i // 2}", f"aK{i // 4}"):
                        pe.wait_ge(gen_read[bank], value)
                    for t in range(T):
                        keys = P * (t + 1)
                        pe.wait_ge(s_masked.sem, s_masked.at(b, 2 * i + t - 1))
                        pe.matmul(s_ps[t][:, 0:2 * keys], q[:, t * P:(t + 1) * P], KB[:, i // 2, :, 0:keys],
                                  start=True, stop=True).then_inc(s_full.sem, 1)

                def probs_transposed(i):
                    pe.wait_ge(p_ready.sem, p_ready.at(b, i + 1))
                    sm = SM[:, i % 2, :]
                    pe.wait_ge(pt0_ready.sem, pt0_ready.at(b, i))
                    for h in range(2):
                        pe.transpose(pt_ps[0][:, h * S:h * S + P], sm[:, h * P:(h + 1) * P], ident[:, :])
                        ins = pe.transpose(pt_ps[0][:, h * S + P:(h + 1) * S],
                                           sm[:, 2 * P + h * S:2 * P + h * S + P], ident[:, :])
                    ins.then_inc(pt_full.sem, 1)
                    pe.wait_ge(pt1_ready.sem, pt1_ready.at(b, i))
                    for h in range(2):
                        ins = pe.transpose(pt_ps[1][:, h * P:(h + 1) * P],
                                           sm[:, 2 * P + h * S + P:2 * P + (h + 1) * S], ident[:, :])
                    ins.then_inc(pt_full.sem, 1)

                def values(i):
                    if i == 0:
                        for bank, value in ph.read("aV0", "aV1"):
                            pe.wait_ge(gen_read[bank], value)
                    pe.wait_ge(pt0_ready.sem, pt0_ready.at(b, i + 1))
                    pe.wait_ge(pt1_ready.sem, pt1_ready.at(b, i + 1))
                    pe.wait_ge(z_low.sem, z_low.at(b, i // 2))
                    at = i % 2 * S
                    pt = PT[:, i % 2, :]
                    for h in range(2):
                        v = slice((i // 2 * 2 + h) * E, (i // 2 * 2 + h + 1) * E)
                        rows = slice(h * E, (h + 1) * E)
                        pe.matmul(z_ps[rows, at:at + S], Vt[:, 0, v], pt[:, h * S:(h + 1) * S],
                                  start=True, stop=False)
                        ins = pe.matmul(z_ps[rows, at + P:at + S], Vt[:, 1, v],
                                        pt[:, 2 * S + h * P:2 * S + (h + 1) * P], start=False, stop=True)
                    ins.then_inc(z_full.sem, 1)

                if ph.attn:
                    pe.wait_ge(xT_high.sem, xT_high.at(b, 1))
                    pe.wait_ge(xT_low.sem, xT_low.at(b, 1))
                    for name in BEFORE:
                        if not ph.rest:
                            pe.wait_ge(w_low.sem, w_low.at(0, {"Q": 2, "K": 3, "V": 4}[name[1]]))
                        fill(name)
                for i in range(STEPS):
                    if ph.attn and i < NP:
                        scores(i)
                    if ph.attn and 1 <= i <= NP:
                        probs_transposed(i - 1)
                    for name in ph.fillers(i):
                        fill(name)
                    if ph.attn and i >= 2:
                        values(i - 2)
                if ph.attn:
                    if not ph.rest:
                        pe.wait_ge(w_low.sem, w_low.at(0, len(weights)))
                        pe.wait_ge(small_in.sem, small_in.at(0, 4))
                        pe.wait_ge(pool_set.sem, pool_set.at(0, SETS + 1))
                    fill("aOUT")

            pe.wait_ge(pool_set.sem, pool_set.at(0, SETS))
            phases(pe, body)

        @block.scalar
        def _(act):
            def copy(o, i):
                return act.activation(o, i, ACT.Copy)

            def split_weight(n):
                act.wait_ge(staged[n % 2].sem, staged[n % 2].at(0, n // 2 + 1))
                copy(weights[n][1][0], stage_of(n)).then_inc(w_high.sem, 1)

            def body(ph):
                b, rb = ph.b, ph.rb

                def gated_high(m):
                    for bank, value in ph.read(f"rFFN{m}"):
                        act.wait_ge(gen_read[bank], value)
                    if m == KH // 2:
                        act.wait_ge(gen_full, ph.full("rDOWN0"))
                    copy(H_s[0][:, m % (KH // 2), :], G[:, m % 2, :]).then_inc(h_high.sem, 1)

                def fill(name):
                    ps = gen[ph.bank(name)]
                    read_out = gen_read[ph.bank(name)]
                    kind, c = name[1:], int(name[-1]) if name[-1].isdigit() else 0
                    if kind[:4] == "DOWN":
                        gated_high(KH // 2 * (c + 1) - 1)
                    if kind[0] == "V" or kind in ("OUT", "XV", "XOUT") or kind[:3] == "SIM" or kind[:4] == "DOWN":
                        return
                    act.wait_ge(gen_full, ph.full(name))
                    if kind[0] == "Q":
                        copy(QT[:, c % 2, :, :], halves_view(ps[:, :])).then_inc(read_out, 1)
                    elif kind[0] == "K":
                        for h in range(2):
                            rows = slice(h * E, (h + 1) * E)
                            ins = copy(KB[rows, 2 * c:2 * c + 2, h, :], halves_view(ps[rows, :]))
                        ins.then_inc(read_out, 1)
                    elif kind[:2] == "T1":
                        act.wait_ge(gen_full, ph.full("rT11"))
                        act.activation(XN[:, c * S:(c + 1) * S], ps[:, 0:S], ACT.Identity, scale=lnw[:, c:c + 1],
                                       bias=lnb[:, c:c + 1]).then_inc(read_out, 1)
                        if c == 1:
                            for bank, value in ph.read("rT10", "rT11"):
                                act.wait_ge(gen_read[bank], value)
                            copy(NT_s[0][:, :, :], halves_view(XN[:, :])).then_inc(nt_high.sem, 1)
                    elif kind == "XK":
                        for h in range(2):
                            rows = slice(h * E, (h + 1) * E)
                            ins = copy(KX[rows, :, h * V:(h + 1) * V],
                                       ps[rows, :].rearrange("p (m v) -> p m v", m=XP)[:, :, 0:V])
                        ins.then_inc(read_out, 1)
                    elif kind[:2] == "XQ":
                        copy(QX_q[:, 2 * c:2 * c + 2, :], halves_view(ps[:, :])).then_inc(read_out, 1)
                    elif kind[:2] == "T2":
                        copy(QX_p[:, 4 * c:4 * c + 4, :], ps[:, :].rearrange("p (h s) -> p h s", h=4))\
                            .then_inc(read_out, 1)
                    elif kind[:3] == "XPV":
                        copy(ZX_s[0][:, :, c * P:(c + 1) * P], ps[:, :].rearrange("p (m s) -> p m s", m=XP))\
                            .then_inc(zx_high.sem, 1)
                    elif kind[:2] == "T3":
                        copy(NT_s[0][:, c, :], ps[:, 0:S]).then_inc(nt_high.sem, 1)
                    elif kind[:3] == "FFN":
                        if c >= 2:
                            act.wait_ge(h_low.sem, h_low.at(rb, c - 1))
                        act.activation(G[:, c % 2, :], ps[:, 0:S], ACT.Tanh, scale=0.5 * QUANT)\
                            .then_inc(tanh_done.sem, 1)
                        if c % (KH // 2) > 0:
                            gated_high(c - 1)

                def exps(i):
                    act.wait_ge(s_masked.sem, s_masked.at(b, 2 * i + 2))
                    sm = SM[:, i % 2, :]
                    for n, (at, keys) in enumerate(((0, P), (P, P), (2 * P, S), (2 * P + S, S))):
                        part = sm[:, at:at + keys]
                        ins = act.activation(part, part, ACT.Exp, scale=-1.0, bias=least[:, i % 2, n:n + 1],
                                             accum_out=total[:, i % 2, n:n + 1])
                    ins.then_inc(exp_done.sem, 1)

                def context_exps(t):
                    act.wait_ge(sx_shifted.sem, sx_shifted.at(rb, t + 1))
                    act.activation(SX[:, :, :], SX[:, :, :], ACT.Exp)
                    act.activation(pmax[:, 2, :], pmax[:, 1, :], ACT.Exp).then_inc(sx_exp.sem, 1)

                if ph.attn:
                    act.wait_ge(xT_loaded.sem, xT_loaded.at(b, 1))
                    copy(xT_s[0][:, :, :], xT_in[:, :, :]).then_inc(xT_high.sem, 1)
                if ph.rest:
                    act.wait_ge(ctx_loaded.sem, ctx_loaded.at(rb, 1))
                    copy(ctx_s[0][:, :, :], ctx_in[:, :, :]).then_inc(ctx_high.sem, 1)
                if ph.attn:
                    for name in BEFORE:
                        fill(name)
                for i in range(STEPS):
                    if ph.attn and 1 <= i <= NP:
                        act.wait_ge(pt_full.sem, pt_full.at(b, 2 * i - 1))
                        act.wait_ge(z_full.sem, z_full.at(b, i - 2))
                        copy(PT[:, (i - 1) % 2, 0:2 * S], pt_ps[0][:, :]).then_inc(pt0_ready.sem, 1)
                    if ph.attn and i < NP:
                        exps(i)
                    for name in ph.fillers(i):
                        fill(name)
                        if name in ("rSIM01", "rSIM11"):
                            context_exps(int(name[4]))
                    if ph.attn and not ph.rest:
                        for n in late_weights[i]:
                            split_weight(n)
                    if ph.attn and i >= 3 and i % 2:
                        m = (i - 3) // 2
                        act.wait_ge(z_full.sem, z_full.at(b, 2 * m + 2))
                        copy(Z_s[0][:, 2 * m:2 * m + 2, :], halves_view(z_ps[:, :])).then_inc(z_high.sem, 1)

            for n in range(EARLY):
                split_weight(n)
            act.wait_ge(pool_set.sem, pool_set.at(0, SETS))
            act.wait_ge(small_in.sem, small_in.at(0, 4))
            phases(act, body)

        @block.vector
        def _(dve):
            def split_weight(n):
                dve.wait_ge(w_high.sem, w_high.at(0, n + 1))
                high, low = weights[n][1]
                dve.tensor_tensor(low, stage_of(n), high.bitcast(F32), ALU.subtract).then_inc(w_low.sem, 1)

            def stand_alone():
                dve.sem_inc(waited, 1)

            def body(ph):
                b, rb = ph.b, ph.rb
                dve_a.begin()
                dve_r.begin()

                def norm(src, dst, chain, batch, moments_ready, rstd_ready, count):
                    for t in range(T):
                        ins = dve.bn_stats(stats[:, t, :], src[:, t, :])
                    ins.then_inc(chain.next(), 1)
                    dve.wait_ge(chain.sem, chain.so_far(batch))
                    stand_alone()
                    for t in range(T):
                        ins = dve.bn_aggr(moments[:, t, :], stats[:, t, :])
                    ins.then_inc(moments_ready.sem, 1)
                    dve.wait_ge(rstd_ready.sem, rstd_ready.at(batch, count))
                    for t in range(T):
                        ins = dve.tensor_scalar(dst[:, t, :], src[:, t, :], moments[:, t, 0:1], rstd[:, t:t + 1],
                                                ALU.subtract, ALU.mult)
                    return ins

                def masks():
                    dve.wait_ge(mask_loaded.sem, mask_loaded.at(rb, 1))
                    dve.tensor_scalar(allowed[:, :, :], mask_in[:, :, :], 0.0, None, ALU.not_equal).then_inc(dve_r.next(), 1)
                    dve.wait_ge(dve_r.sem, dve_r.so_far(rb))
                    for t in range(T):
                        ins = dve.tensor_tensor_scan(taken[:, t, :], ones[:, 0:V], allowed[:, t, :], 0.0,
                                                     ALU.mult, ALU.add)
                    ins.then_inc(dve_r.next(), 1)
                    dve.wait_ge(dve_r.sem, dve_r.so_far(rb))
                    found = taken[:, :, V - 1]
                    dve.tensor_scalar(count[:, :, 0], found, -1.0, float(TOP), ALU.mult, ALU.add)
                    dve.tensor_scalar(count[:, :, 1], found, float(TOP), NEG, ALU.is_ge, ALU.mult).then_inc(dve_r.next(), 1)
                    dve.wait_ge(dve_r.sem, dve_r.so_far(rb))
                    dve.tensor_scalar(count[:, :, 0], count[:, :, 0], 0.0, None, ALU.max)
                    dve.tensor_scalar(pad_bias[:, :], count[:, :, 1], PAD_BIAS, None, ALU.add)
                    dve.scalar_tensor_tensor(out=taken[:, :, :], in0=taken[:, :, :], scalar=float(TOP),
                                                        in1=allowed[:, :, :], op0=ALU.is_le, op1=ALU.mult).then_inc(dve_r.next(), 1)
                    dve.wait_ge(dve_r.sem, dve_r.so_far(rb))
                    dve.tensor_scalar(taken[:, :, :], taken[:, :, :], -1.0, -NEG, ALU.add, ALU.mult)\
                        .then_inc(mask_read.sem, 1)

                def context_shift(t):
                    for bank, value in ph.read(f"rSIM{t}0", f"rSIM{t}1"):
                        dve.wait_ge(gen_read[bank], value)
                    dve.tensor_reduce(pmax[:, 0, :], SX[:, :, :], AX_X, ALU.max).then_inc(dve_r.next(), 1)
                    dve.wait_ge(dve_r.sem, dve_r.so_far(rb))
                    dve.tensor_scalar(pmax[:, 0, :], pmax[:, 0, :], pad_bias[:, t:t + 1], None, ALU.max).then_inc(dve_r.next(), 1)
                    dve.wait_ge(dve_r.sem, dve_r.so_far(rb))
                    dve.tensor_scalar(pmax[:, 1, :], pmax[:, 0, :], -1.0, pad_bias[:, t:t + 1], ALU.mult, ALU.add)
                    dve.tensor_tensor(SX[:, :, :], SX[:, :, :], pmax[:, 0, :].unsqueeze(2).broadcast_to([P, XH, V]),
                                      ALU.subtract).then_inc(sx_shifted.sem, 1)

                def context_probs(t):
                    dve.wait_ge(sx_exp.sem, sx_exp.at(rb, t + 1))
                    dve.tensor_reduce(den[:, 0, :], SX[:, :, :], AX_X, ALU.add).then_inc(dve_r.next(), 1)
                    dve.wait_ge(dve_r.sem, dve_r.so_far(rb))
                    dve.scalar_tensor_tensor(out=den[:, 1, :], in0=pmax[:, 2, :], scalar=count[:, t, 0:1],
                                                        in1=den[:, 0, :], op0=ALU.mult, op1=ALU.add).then_inc(dve_r.next(), 1)
                    dve.wait_ge(dve_r.sem, dve_r.so_far(rb))
                    dve.reciprocal(den[:, 0, :], den[:, 1, :]).then_inc(dve_r.next(), 1)
                    dve.wait_ge(dve_r.sem, dve_r.so_far(rb))
                    if t > 0:
                        dve.wait_ge(gen_full, ph.full(f"rT2{t - 1}1"))
                    dve.tensor_tensor(PX[:, :, 0:V], SX[:, :, :], den[:, 0, :].unsqueeze(2).broadcast_to([P, XH, V]),
                                      ALU.mult).then_inc(px_ready.sem, 1)

                def fill(name):
                    ps = gen[ph.bank(name)]
                    two = halves_view(ps[:, :])
                    read_out = gen_read[ph.bank(name)]
                    kind, c = name[1:], int(name[-1]) if name[-1].isdigit() else 0
                    if kind[0] == "V":
                        dve.wait_ge(gen_full, ph.full(name))
                        dve.tensor_copy(Vt[:, c, :], ps[:, :]).then_inc(read_out, 1)
                    elif kind == "OUT":
                        dve.wait_ge(x_biased.sem, x_biased.at(b, 1))
                        dve.wait_ge(gen_full, ph.full(name))
                        dve.tensor_tensor(X[:, :, :], two, x_in[:, :, :], ALU.add).then_inc(read_out, 1)
                    elif kind == "T11":
                        dve.wait_ge(nt_high.sem, nt_high.at(rb, 1))
                        dve.tensor_tensor(NT_s[1][:, :, :], halves_view(XN[:, :]), NT_s[0][:, :, :].bitcast(F32),
                                          ALU.subtract).then_inc(nt_low.sem, 1)
                    elif kind == "XV":
                        dve.wait_ge(gen_full, ph.full(name))
                        dve.tensor_copy(VX[:, :], ps[:, :]).then_inc(read_out, 1)
                    elif kind[:3] == "SIM":
                        t = int(kind[3])
                        if t > 0:
                            dve.wait_ge(px_ready.sem, px_ready.at(rb, t))
                        dve.wait_ge(gen_full, ph.full(name))
                        dve.scalar_tensor_tensor(out=SX[:, 4 * c:4 * c + 4, :],
                                                 in0=ps[:, 0:4 * V].rearrange("p (h v) -> p h v", h=4), scalar=SCALE,
                                                 in1=taken[:, t, :].unsqueeze(1).broadcast_to([P, 4, V]),
                                                 op0=ALU.mult, op1=ALU.add).then_inc(read_out, 1)
                    elif kind[:3] == "XPV":
                        dve.wait_ge(zx_high.sem, zx_high.at(rb, c + 1))
                        cols = slice(c * P, (c + 1) * P)
                        dve.tensor_tensor(ZX_s[1][:, :, cols], ps[:, :].rearrange("p (m s) -> p m s", m=XP),
                                          ZX_s[0][:, :, cols].bitcast(F32), ALU.subtract).then_inc(read_out, 1)
                    elif kind == "XOUT":
                        dve.wait_ge(gen_full, ph.full(name))
                        dve.tensor_tensor(X[:, :, :], two, X[:, :, :], ALU.add).then_inc(read_out, 1)
                        for bank, value in ph.read(name):
                            dve.wait_ge(gen_read[bank], value)
                        norm(X, X, dve_r, rb, moments_r, rstd_r, 1).then_inc(x2_ready.sem, 1)
                    elif kind[:2] == "T3":
                        dve.wait_ge(nt_high.sem, nt_high.at(rb, 2 + c))
                        dve.tensor_tensor(NT_s[1][:, c, :], ps[:, 0:S], NT_s[0][:, c, :].bitcast(F32),
                                          ALU.subtract).then_inc(read_out, 1)
                    elif kind[:3] == "FFN":
                        dve.wait_ge(tanh_done.sem, tanh_done.at(rb, c + 1))
                        g = G[:, c % 2, :]
                        dve.scalar_tensor_tensor(out=g, in0=g, scalar=1.0, in1=ps[:, 0:S],
                                                            op0=ALU.add, op1=ALU.mult).then_inc(dve_r.next(), 1)
                        dve.wait_ge(dve_r.sem, dve_r.so_far(rb))
                        dve.tensor_tensor(g, ps[:, S:2 * S], g, ALU.mult).then_inc(read_out, 1)
                    elif kind[:4] == "DOWN":
                        dve.wait_ge(gen_full, ph.full(name))
                        dve.scalar_tensor_tensor(out=XN[:, :], in0=ps[:, :], scalar=0.5 * QUANT ** 3,
                                                 in1=(X[:, :, :].rearrange("p t d -> p (t d)") if c == 0
                                                      else XN[:, :]), op0=ALU.mult, op1=ALU.add)\
                            .then_inc(read_out, 1)
                        for bank, value in ph.read(name):
                            dve.wait_ge(gen_read[bank], value)
                        if c == 1:
                            norm(XN_t, XN_t, dve_r, rb, moments_r, rstd_r, 2).then_inc(out_ready.sem, 1)

                def masked(i):
                    dve.wait_ge(pt_full.sem, pt_full.at(b, 2 * i - 2))
                    for t in range(T):
                        keys = P * (t + 1)
                        dve.wait_ge(s_full.sem, s_full.at(b, 2 * i + t + 1))
                        stand_alone()
                        for h in range(2):
                            at = 2 * P * t + h * keys
                            ins = dve.tensor_tensor_reduce(SM[:, i % 2, at:at + keys],
                                                           s_ps[t][:, h * keys:(h + 1) * keys],
                                                           causal[:, S - keys:S], -SCALE, -3 * NEG, ALU.add, ALU.min,
                                                           least[:, i % 2, 2 * t + h:2 * t + h + 1])
                        ins.then_inc(s_masked.sem, 1)

                def normalised(i):
                    dve.wait_ge(exp_done.sem, exp_done.at(b, i + 1))
                    dve.reciprocal(total[:, i % 2, :], total[:, i % 2, :]).then_inc(dve_a.next(), 1)
                    dve.wait_ge(dve_a.sem, dve_a.so_far(b))
                    for n, (at, keys) in enumerate(((0, P), (P, P), (2 * P, S), (2 * P + S, S))):
                        part = SM[:, i % 2, at:at + keys]
                        ins = dve.tensor_scalar(part, part, total[:, i % 2, n:n + 1], None, ALU.mult)
                    ins.then_inc(p_ready.sem, 1)

                if ph.rest:
                    masks()
                if ph.attn:
                    for name in BEFORE:
                        fill(name)
                for i in range(STEPS):
                    if ph.attn and 1 <= i <= NP:
                        normalised(i - 1)
                    if ph.attn and i < NP:
                        masked(i)
                    if ph.attn and 1 <= i <= NP:
                        dve.wait_ge(pt_full.sem, pt_full.at(b, 2 * i))
                        dve.wait_ge(z_full.sem, z_full.at(b, i - 2))
                        dve.tensor_copy(PT[:, (i - 1) % 2, 2 * S:PAIR], pt_ps[1][:, 0:2 * P]).then_inc(pt1_ready.sem, 1)
                    if ph.rest and i in (3, 5):
                        context_probs((i - 3) // 2)
                    for name in ph.fillers(i):
                        fill(name)
                        if name in ("rSIM01", "rSIM11"):
                            context_shift(int(name[4]))
                    if ph.attn and not ph.rest:
                        for n in late_weights[i]:
                            split_weight(n)
                    if ph.attn and i >= 3 and i % 2:
                        m = (i - 3) // 2
                        dve.wait_ge(z_high.sem, z_high.at(b, m + 1))
                        pairs = slice(2 * m, 2 * m + 2)
                        dve.tensor_tensor(Z_s[1][:, pairs, :], halves_view(z_ps[:, :]),
                                          Z_s[0][:, pairs, :].bitcast(F32), ALU.subtract).then_inc(z_low.sem, 1)
                if ph.attn:
                    fill("aOUT")
                    for bank, value in ph.read("aOUT"):
                        dve.wait_ge(gen_read[bank], value)
                    norm(X, X, dve_a, b, moments_a, rstd_a, 1).then_inc(dve_a.next(), 1)
                    dve.wait_ge(dve_a.sem, dve_a.so_far(b))
                    dve.wait_ge(out_stored.sem, out_stored.at(b, 0))
                    norm(X, XN_t, dve_a, b, moments_a, rstd_a, 2).then_inc(xn_ready.sem, 1)
                    if not ph.rest:
                        dve.wait_ge(pool_set.sem, pool_set.at(0, SETS + 1))
                    dve_a.end()
                if ph.rest:
                    dve_r.end()

            for n in range(EARLY):
                split_weight(n)
            dve.wait_ge(pool_set.sem, pool_set.at(0, SETS))
            phases(dve, body)

        @block.gpsimd
        def _(pool):
            def body(ph):
                b, rb = ph.b, ph.rb
                pool_a.begin()
                pool_r.begin()

                def inverse_deviation(chain, batch, moments_ready, rstd_ready, count):
                    pool.wait_ge(moments_ready.sem, moments_ready.at(batch, count))
                    pool.tensor_tensor(var[:, :], moments[:, :, 1], eps[:, :], ALU.add).then_inc(chain.next(), 1)
                    pool.wait_ge(chain.sem, chain.so_far(batch))
                    pool.tensor_tensor(rstd[:, :], var[:, :], minus_half[:, :], ALU.pow).then_inc(rstd_ready.sem, 1)

                if ph.attn:
                    pool.wait_ge(xT_high.sem, xT_high.at(b, 1))
                    pool.tensor_tensor(xT_s[1][:, :, :], xT_in[:, :, :], xT_s[0][:, :, :].bitcast(F32),
                                       ALU.subtract).then_inc(xT_low.sem, 1)
                if ph.rest:
                    pool.wait_ge(ctx_high.sem, ctx_high.at(rb, 1))
                    pool.tensor_tensor(ctx_s[1][:, :, :], ctx_in[:, :, :], ctx_s[0][:, :, :].bitcast(F32),
                                       ALU.subtract).then_inc(ctx_low.sem, 1)
                if ph.attn:
                    pool.wait_ge(x_loaded.sem, x_loaded.at(b, 1))
                    pool.tensor_tensor(x_in[:, :, :], x_in[:, :, :], bias[:, :].unsqueeze(1).broadcast_to([P, T, D]),
                                       ALU.add).then_inc(x_biased.sem, 1)
                if ph.attn and not ph.rest:
                    pool.wait_ge(w_low.sem, w_low.at(0, len(weights)))
                    pool.memset(PX[:, :, :], 0.0).then_inc(pool_set.sem, 1)
                if ph.rest:
                    inverse_deviation(pool_r, rb, moments_r, rstd_r, 1)
                    for m in range(KH):
                        pool.wait_ge(h_high.sem, h_high.at(rb, m + 1))
                        slot = m % (KH // 2)
                        pool.tensor_tensor(H_s[1][:, slot, :], G[:, m % 2, :], H_s[0][:, slot, :].bitcast(F32),
                                           ALU.subtract).then_inc(h_low.sem, 1)
                    inverse_deviation(pool_r, rb, moments_r, rstd_r, 2)
                if ph.attn:
                    inverse_deviation(pool_a, b, moments_a, rstd_a, 1)
                    inverse_deviation(pool_a, b, moments_a, rstd_a, 2)

            zeros = [ident, ctx_in, KB, causal, KX]
            for z in zeros:
                pool.memset(z[tuple([slice(None)] * len(z.shape))], 0.0).then_inc(pool_set.sem, 1)
            pool.memset(ones[:, :], 1.0).then_inc(pool_set.sem, 1)
            pool.memset(minus_half[:, :], -0.5).then_inc(pool_set.sem, 1)
            pool.memset(eps[:, :], EPS).then_inc(pool_set.sem, 1)
            pool.wait_ge(pool_set.sem, pool_set.at(0, 8))
            pool.affine_select(out=ident[:, :], in_=ident[:, :], compare_op=ALU.not_equal, fill=1.0, base=0,
                               pattern=[[-1, P]], channel_multiplier=1).then_inc(pool_set.sem, 1)
            pool.affine_select(out=causal[:, P:S], in_=causal[:, P:S], compare_op=ALU.is_ge, fill=NEG, base=0,
                               pattern=[[-1, P]], channel_multiplier=1).then_inc(pool_set.sem, 1)
            pool.wait_ge(small_in.sem, small_in.at(0, 4))
            phases(pool, body)


_ORDER = ["x", "xT", "ctxT", "maskT", "wq", "wk", "wv", "wo", "b_out", "ln_w", "ln_b", "xwq", "xwkv", "xwo",
          "wg", "wu", "wd"]


def kernel(x, ctx_1024, mask_BxS2xS_ik0, L0_attn_W_Q, L0_attn_W_K, L0_attn_W_V, L0_attn_W_out, L0_attn_b_out,
           L0_xattn_ln_w, L0_xattn_ln_b, L0_xattn_Wq, L0_xattn_Wkv, L0_xattn_Wout, L0_ffn_w_gate, L0_ffn_w_up,
           L0_ffn_w_down):
    import numpy as np
    import concourse.bacc as bacc
    from concourse.bass_utils import run_bass_kernel_spmd

    def lay(a, *axes):
        return np.ascontiguousarray(np.transpose(np.asarray(a), axes))

    D, NH, E = L0_attn_W_Q.shape
    pairs = (NH // 4, 2, 2)
    wq = lay(np.asarray(L0_attn_W_Q).reshape(D, *pairs, E), 0, 1, 3, 2, 4).reshape(D, NH * E)
    wo = lay(np.asarray(L0_attn_W_out).reshape(E, *pairs, D), 1, 3, 2, 0, 4).reshape(NH * E, D)
    arrays = {
        "x": lay(x, 0, 1, 2), "xT": lay(x, 0, 2, 1), "ctxT": lay(ctx_1024, 0, 2, 1),
        "maskT": lay(mask_BxS2xS_ik0, 0, 2, 1),
        "wq": wq, "wk": lay(L0_attn_W_K, 0, 1, 2).reshape(D, -1), "wv": lay(L0_attn_W_V, 0, 1, 2).reshape(D, -1),
        "wo": wo, "b_out": lay(L0_attn_b_out, 0), "ln_w": lay(np.asarray(L0_xattn_ln_w).reshape(-1, P), 1, 0),
        "ln_b": lay(np.asarray(L0_xattn_ln_b).reshape(-1, P), 1, 0),
        "xwq": lay(L0_xattn_Wq, 0, 1), "xwkv": lay(L0_xattn_Wkv, 0, 1), "xwo": lay(L0_xattn_Wout, 0, 1),
        "wg": lay(L0_ffn_w_gate, 1, 0), "wu": lay(L0_ffn_w_up, 1, 0), "wd": lay(L0_ffn_w_down, 1, 0),
    }
    nc = bacc.Bacc("TRN2", target_bir_lowering=False, num_devices=1)
    inputs = {f"in_{n}": arrays[n] for n in _ORDER}
    args = [nc.dram_tensor(n, a.shape, mybir.dt.from_np(a.dtype), kind="ExternalInput").ap()
            for n, a in inputs.items()]
    out = nc.dram_tensor("out", x.shape, F32, kind="ExternalOutput").ap()
    decoder_layer(nc, *args, out)
    r = run_bass_kernel_spmd(nc, [inputs], core_ids=[0])
    return r.results[0]["out"]
```

```python
from contextlib import ExitStack

import concourse.bass as bass
from concourse import mybir

F32 = mybir.dt.float32
F32R = mybir.dt.float32r
I32 = mybir.dt.int32
ALU = mybir.AluOpType
ACT = mybir.ActivationFunctionType
AX_X = mybir.AxisListType.X

P = 128
EPS = 1e-5
NEG = -1e30
PAD_BIAS = -10000.0
TOP = 5
QUANT = 1.0 / 127.0


class Signal:

    def __init__(self, nc, ctx, name, per_batch, unit=1):
        self.sem = ctx.enter_context(nc.semaphore(name))
        self.per_batch = per_batch
        self.unit = unit

    def at(self, batch, count):
        value = (batch * self.per_batch + count) * self.unit
        return max(value, 0) if isinstance(value, int) else value


class Chain:

    def __init__(self, nc, ctx, name, per_batch):
        self.sem = ctx.enter_context(nc.semaphore(name))
        self.per_batch = per_batch
        self.n = 0

    def begin(self):
        self.n = 0

    def next(self):
        self.n += 1
        return self.sem

    def so_far(self, batch):
        return batch * self.per_batch + self.n

    def end(self):
        assert self.n == self.per_batch, (self.n, self.per_batch)


T_LAG, P_LAG = 2, 3
SEQUENCE = [
    ["S", "rXK", "rT10", "rT11"],
    ["S", "aQ2", "rXV"],
    ["T", "S", "rXQ0", "rXQ1"],
    ["T", "S", "rSIM00", "rSIM01", "P", "aQ3"],
    ["T", "S", "rSIM10", "rSIM11", "P"],
    ["T", "S", "rT200", "rT201", "P"],
    ["T", "S", "rXPV0", "rT210", "rT211", "P"],
    ["T", "S", "rXPV1", "P", "nQ0"],
    ["T", "nK0", "rXOUT", "P", "nQ1"],
    ["T", "nK1", "rT30", "rT31", "P", "rFFN0", "rFFN1"],
    ["P", "rFFN2", "rFFN3", "nV0", "rDOWN0", "rFFN4", "rFFN5", "aOUT", "nV1", "rDOWN1"],
]
BANKS = 3


class Phase:

    def __init__(self, b, parts, turn):
        self.b, self.rb, self.turn = b, b - 1, turn
        self.attn, self.rest, self.next = "a" in parts, "r" in parts, "n" in parts
        names = [n for step in SEQUENCE for n in step if n[0] in parts]
        assert len(names) % BANKS == 0
        self.turns = len(names) // BANKS
        self.index = {n: i for i, n in enumerate(names)}

    def step(self, i):
        pair = {"S": i, "T": i - T_LAG, "P": i - P_LAG}
        return [(n, pair.get(n)) for n in SEQUENCE[i] if n in self.index or (n in pair and self.attn)]

    def bank(self, name):
        return self.index[name] % BANKS

    def full(self, name):
        return self.turn * BANKS + self.index[name] + 1

    def read(self, *names, before=None):
        counts = {}
        for name in names + (before,) * (before is not None):
            turns = self.index[name] // BANKS + (name != before)
            counts[self.bank(name)] = max(turns, counts.get(self.bank(name), 0))
        return [(bank, self.turn + turns) for bank, turns in counts.items()]


def decoder_layer(nc, x, xT, ctxT, maskT, wq, wk, wv, wo, b_out, ln_w, ln_b, xwq, xwkv, xwo, wg, wu, wd, out):
    B, S, D = x.shape
    V = ctxT.shape[2]
    KD = D // P
    T = S // P
    HE = wq.shape[1]
    KE = wk.shape[1]
    E = 64
    NP = HE // P
    NJ = KE // P
    XE = xwq.shape[1]
    XP = XE // P
    XH = XE // E
    HID = wg.shape[1]
    KH = HID // P
    SCALE = E ** -0.5
    NORMS = 4
    PAIR = T * S + T * P

    def phases(eng, body):
        start = Phase(-1, "n", 0)
        first = Phase(0, "an", start.turns)
        full = Phase(1, "arn", start.turns + first.turns)
        last = Phase(B - 1, "ar", full.turn + (B - 2) * full.turns)
        end = Phase(B, "r", last.turn + last.turns)
        body(start)
        body(first)
        with eng.Fori(1, B - 1) as b:
            body(Phase(b, "arn", b * full.turns + (full.turn - full.turns)))
        body(last)
        body(end)

    with ExitStack() as ctx:
        def sb(name, shape, dt=F32):
            return ctx.enter_context(nc.sbuf_tensor(name, shape, dt))

        def signal(name, per_batch, unit=1):
            return Signal(nc, ctx, name, per_batch, unit)

        def halves(name, shape):
            return sb(name + "_hi", shape, F32R), sb(name + "_lo", shape, F32R)

        wq_s = halves("wq", [P, KD, HE])
        wk_s = halves("wk", [P, KD, KE])
        wv_s = halves("wv", [P, KD, KE])
        wo_s = halves("wo", [P, NP, D])
        xwq_s = halves("xwq", [P, KD, XE])
        xwk = sb("xwk", [P, KD, XE])
        xwv_s = halves("xwv", [P, KD, XE])
        xwo_s = halves("xwo", [P, XP, D])
        wg_s = halves("wg", [P, KD, HID])
        wu_s = halves("wu", [P, KD, HID])
        wd_s = halves("wd", [P, KH, D])
        lnw = sb("lnw", [P, KD])
        lnb = sb("lnb", [P, KD])
        bias = sb("bias", [P, D])
        ident = sb("ident", [P, P])
        causal = sb("causal", [P, S])
        ones = sb("ones", [P, V])
        minus_half = sb("minus_half", [P, T])
        eps = sb("eps", [P, T])

        x_in = sb("x_in", [P, T, D])
        xT_in = sb("xT_in", [P, KD, S])
        xT_s = halves("xTs", [P, KD, S])
        QT = sb("QT", [P, 2, 2, S])
        KB = sb("KB", [P, NJ, 2, S])
        Vt = sb("Vt", [P, T, KE])
        SM = sb("SM", [P, 2, PAIR])
        least = sb("least", [P, 2, 4])
        total = sb("total", [P, 2, 4])
        PT = sb("PT", [P, 2, PAIR])
        Z_s = halves("Z", [P, NP, S])

        X = sb("X", [P, T, D])
        XN = sb("XN", [P, T * D])
        XN_t = XN[:, :].rearrange("p (t d) -> p t d", t=T)
        Y = sb("Y", [P, T, D])
        NT_s = halves("NT", [P, KD, S])
        stats = sb("stats", [P, NORMS, T, 6])
        moments = sb("moments", [P, NORMS, T, 2])
        var = sb("var", [P, NORMS, T])
        rstd = sb("rstd", [P, NORMS, T])
        ctx_in = sb("ctx_in", [P, KD, P])
        ctx_s = halves("ctxs", [P, KD, P])
        mask_in = sb("mask_in", [P, T, V], I32)
        allowed = sb("allowed", [P, T, V])
        taken = sb("taken", [P, T, V])
        count = sb("count", [P, T, 2])
        pad_bias = sb("pad_bias", [P, T])
        KX = sb("KX", [P, XP, 2 * V])
        VX = sb("VX", [P, XE])
        SX = sb("SX", [P, XH, V])
        PX = sb("PX", [P, XH, P])
        pmax = sb("pmax", [P, 3, XH])
        den = sb("den", [P, 2, XH])
        QX = sb("QX", [P, XH * P])
        QX_q = QX[:, :].rearrange("p (c s) -> p c s", c=XP)
        QX_p = QX[:, :].rearrange("p (h s) -> p h s", h=XH)
        G = sb("G", [P, 2, S])
        H_s = halves("H", [P, KH // 2, S])
        ZX_s = [z[:, NP - XP:NP, :] for z in Z_s]

        stage = [PX[:, :, :].rearrange("p h s -> p (h s)"), QX[:, :]]

        def bank(name):
            return ctx.enter_context(nc.psum_tensor(name, [P, 512], F32))

        gen = [bank(f"gen{i}") for i in range(BANKS)]
        s_ps = [bank(f"s_ps{i}") for i in range(2)]
        pt_ps = [bank(f"pt_ps{i}") for i in range(2)]
        z_ps = bank("z_ps")

        staged = [signal(f"staged{i}", 0, 16) for i in range(2)]
        w_high = signal("w_high", 0)
        w_low = signal("w_low", 0)
        small_in = signal("small_in", 0, 16)
        pool_set = signal("pool_set", 0)
        xT_loaded = signal("xT_loaded", 1, 16)
        x_loaded = signal("x_loaded", 1, 16)
        ctx_loaded = signal("ctx_loaded", 1, 16)
        mask_loaded = signal("mask_loaded", 1, 16)
        y_free = signal("y_free", 1, 16)
        gen_full = ctx.enter_context(nc.semaphore("gen_full"))
        gen_read = [ctx.enter_context(nc.semaphore(f"gen_read{i}")) for i in range(BANKS)]
        xT_high = signal("xT_high", 1)
        xT_low = signal("xT_low", 1)
        x_biased = signal("x_biased", 1)
        s_full = signal("s_full", 2 * NP)
        s_masked = signal("s_masked", 2 * NP)
        exp_done = signal("exp_done", NP)
        p_ready = signal("p_ready", NP)
        pt_full = signal("pt_full", 2 * NP)
        pt0_ready = signal("pt0_ready", NP)
        pt1_ready = signal("pt1_ready", NP)
        z_full = signal("z_full", NP)
        z_high = signal("z_high", NP // 2)
        z_low = signal("z_low", NP // 2)
        xn_ready = signal("xn_ready", 1)
        moments_a = signal("moments_a", 2)
        rstd_a = signal("rstd_a", 2)
        dve_a = Chain(nc, ctx, "dve_a", NP + 3)
        pool_a = Chain(nc, ctx, "pool_a", 2)
        moments_r = signal("moments_r", 2)
        rstd_r = signal("rstd_r", 2)
        nt_high = signal("nt_high", 3)
        nt_low = signal("nt_low", 1)
        ctx_high = signal("ctx_high", 1)
        ctx_low = signal("ctx_low", 1)
        mask_read = signal("mask_read", 1)
        sx_shifted = signal("sx_shifted", 2)
        sx_exp = signal("sx_exp", 2)
        px_ready = signal("px_ready", 2)
        zx_high = signal("zx_high", 2)
        x2_ready = signal("x2_ready", 1)
        tanh_done = signal("tanh_done", KH)
        h_high = signal("h_high", KH)
        h_low = signal("h_low", KH)
        out_ready = signal("out_ready", 1)
        waited = ctx.enter_context(nc.semaphore("waited"))
        dve_r = Chain(nc, ctx, "dve_r", 22)
        pool_r = Chain(nc, ctx, "pool_r", 2)

        weights = []
        for w, parts, per in ((wq, wq_s, 1), (wk, wk_s, 2), (wv, wv_s, 2), (wo, wo_s, 4), (xwkv[:, XE:], xwv_s, 2),
                              (xwq, xwq_s, 2), (xwo, xwo_s, 4), (wg, wg_s, 1), (wu, wu_s, 1), (wd, wd_s, 3)):
            rows = w.rearrange("(k p) n -> p k n", p=P)
            for k in range(0, rows.shape[1], per):
                weights.append((rows[:, k:k + per, :], [part[:, k:k + per, :] for part in parts], per, rows.shape[2]))

        def stage_of(n):
            _, _, per, cols = weights[n]
            flat = stage[n % 2][:, 0:per * cols].rearrange("p (k n) -> p k n", k=per)
            return flat if weights[n][0].dtype == F32 else flat.bitcast(I32)

        EARLY = 4
        late_weights = [[] for _ in SEQUENCE]
        for n in range(EARLY, len(weights)):
            late_weights[(n - EARLY) * (len(SEQUENCE) - 2) // (len(weights) - EARLY)].append(n)
        SETS = 10

        def halves_view(t):
            return t.rearrange("p (c s) -> p c s", c=2)

        block = ctx.enter_context(nc.Block())

        @block.sync
        def _(sp):
            def load_xT(b):
                sp.wait_ge(xT_high.sem, xT_high.at(b, 0))
                sp.wait_ge(xT_low.sem, xT_low.at(b, 0))
                sp.dma_start(xT_in[:, :, :], xT[b].rearrange("(k p) s -> p k s", p=P)).then_inc(xT_loaded.sem, 16)

            def load_x(b):
                sp.wait_ge(moments_a.sem, moments_a.at(b, -1))
                sp.dma_start(x_in[:, :, :], x[b].rearrange("(t p) d -> p t d", p=P)).then_inc(x_loaded.sem, 16)

            def load_ctx(b):
                if not isinstance(b, int) or b > 0:
                    sp.wait_ge(s_full.sem, s_full.at(b, 5))
                sp.dma_start(ctx_in[:, :, 0:V], ctxT[b].rearrange("(k p) v -> p k v", p=P)).then_inc(ctx_loaded.sem, 16)
                sp.wait_ge(mask_read.sem, mask_read.at(b, 0))
                sp.dma_start(mask_in[:, :, :], maskT[b].rearrange("(t p) v -> p t v", p=P)).then_inc(mask_loaded.sem, 16)

            def store(b):
                sp.wait_ge(out_ready.sem, out_ready.at(b, 1))
                sp.dma_start(out[b].rearrange("(t p) d -> p t d", p=P), Y[:, :, :]).then_inc(y_free.sem, 16)

            load_xT(0)
            for n in range(len(weights)):
                if n >= 2:
                    sp.wait_ge(w_low.sem, n - 1)
                sp.dma_start(stage_of(n), weights[n][0]).then_inc(staged[n % 2].sem, 16)
                if n == 1:
                    sp.dma_start(bias[:, :], b_out.partition_broadcast(P)).then_inc(small_in.sem, 16)
                    sp.dma_start(lnw[:, :], ln_w).then_inc(small_in.sem, 16)
                    sp.dma_start(lnb[:, :], ln_b).then_inc(small_in.sem, 16)
                    sp.dma_start(xwk[:, :, :], xwkv[:, 0:XE].rearrange("(k p) n -> p k n", p=P)).then_inc(small_in.sem, 16)
                    load_x(0)
                if n == EARLY:
                    load_xT(1)
                    sp.wait_ge(pool_set.sem, SETS)
                    load_ctx(0)
            load_x(1)
            with sp.Fori(1, B - 1) as b:
                load_xT(b + 1)
                load_ctx(b)
                load_x(b + 1)
                store(b - 1)
            load_ctx(B - 1)
            store(B - 2)
            store(B - 1)
            sp.wait_ge(y_free.sem, y_free.at(B, 1))

        @block.tensor
        def _(pe):
            def split_product(o, left, right, first=True, last=True):
                pe.matmul(o, left[0], right[0], start=first, stop=False)
                pe.matmul(o, left[0], right[1], start=False, stop=False)
                return pe.matmul(o, left[1], right[0], start=False, stop=last)

            def project(o, left, right, k_tiles):
                for k in range(k_tiles):
                    ins = split_product(o, left(k), right(k), k == 0, k == k_tiles - 1)
                return ins

            def tile_of(parts, cols):
                return lambda k: [part[:, k, cols] for part in parts]

            def body(ph):
                b, rb = ph.b, ph.rb
                whole = slice(None)

                def inputs_of(name):
                    kind, last = name[1:], name[-1]
                    if kind[:3] == "SIM":
                        return f"rXQ{last}", "rXK"
                    if kind[:3] == "XPV":
                        return "rXV", f"rT2{last}0", f"rT2{last}1"
                    if kind == "XOUT":
                        return "rXPV0", "rXPV1"
                    if kind[:3] == "FFN":
                        return "rT30", "rT31"
                    return ()

                def fill(name):
                    for bank, value in ph.read(*inputs_of(name), before=name):
                        pe.wait_ge(gen_read[bank], value)
                    ps = gen[ph.bank(name)]
                    two = halves_view(ps[:, :])
                    kind, c = name[1:], int(name[-1]) if name[-1].isdigit() else 0
                    if kind[0] in "QK":
                        parts = wq_s if kind[0] == "Q" else wk_s
                        for i in range(2):
                            m = slice((2 * c + i) * P, (2 * c + i + 1) * P)
                            ins = project(two[:, i, :], tile_of(parts, m), tile_of(xT_s, whole), KD)
                    elif kind[0] == "V":
                        ins = project(ps[:, :], tile_of(xT_s, slice(c * P, (c + 1) * P)), tile_of(wv_s, whole), KD)
                    elif kind == "OUT":
                        pe.wait_ge(z_low.sem, z_low.at(b, NP // 2))
                        for t in range(T):
                            ins = project(two[:, t, :], tile_of(Z_s, slice(t * P, (t + 1) * P)),
                                          tile_of(wo_s, whole), NP)
                    elif kind[:2] == "T1":
                        pe.wait_ge(xn_ready.sem, xn_ready.at(rb, 1))
                        for t in range(T):
                            ins = pe.transpose(ps[:, t * P:(t + 1) * P], XN_t[:, t, c * P:(c + 1) * P], ident[:, :])
                    elif kind == "XK":
                        pe.wait_ge(ctx_loaded.sem, ctx_loaded.at(rb, 1))
                        for m in range(XP):
                            for k in range(KD):
                                ins = pe.matmul(ps[:, m * P:(m + 1) * P], xwk[:, k, m * P:(m + 1) * P],
                                                ctx_in[:, k, :], start=(k == 0), stop=(k == KD - 1))
                    elif kind == "XV":
                        pe.wait_ge(ctx_low.sem, ctx_low.at(rb, 1))
                        ins = project(ps[:, :], tile_of(ctx_s, whole), tile_of(xwv_s, whole), KD)
                    elif kind[:2] == "XQ":
                        pe.wait_ge(nt_low.sem, nt_low.at(rb, 1))
                        for i in range(2):
                            m = slice((2 * c + i) * P, (2 * c + i + 1) * P)
                            ins = project(two[:, i, :], tile_of(xwq_s, m), tile_of(NT_s, whole), KD)
                    elif kind[:3] == "SIM":
                        t = int(kind[3])
                        for i in range(2):
                            p = 2 * c + i
                            ins = pe.matmul(ps[:, i * 2 * V:(i + 1) * 2 * V], QX_q[:, p, t * P:(t + 1) * P],
                                            KX[:, p, :], start=True, stop=True)
                    elif kind[:2] == "T2":
                        t = int(kind[2])
                        pe.wait_ge(px_ready.sem, px_ready.at(rb, t + 1))
                        for i in range(4):
                            ins = pe.transpose(ps[:, i * P:(i + 1) * P], PX[:, 4 * c + i, :], ident[:, :])
                    elif kind[:3] == "XPV":
                        for h in range(XH):
                            ins = pe.matmul(ps[E * (h % 2):E * (h % 2 + 1), h // 2 * P:(h // 2 + 1) * P],
                                            VX[:, h * E:(h + 1) * E], QX_p[:, h, :], start=True, stop=True)
                    elif kind == "XOUT":
                        for t in range(T):
                            ins = project(two[:, t, :], tile_of(ZX_s, slice(t * P, (t + 1) * P)),
                                          tile_of(xwo_s, whole), XP)
                    elif kind[:2] == "T3":
                        pe.wait_ge(x2_ready.sem, x2_ready.at(rb, 1))
                        for t in range(T):
                            ins = pe.transpose(ps[:, t * P:(t + 1) * P], X[:, t, c * P:(c + 1) * P], ident[:, :])
                    elif kind[:3] == "FFN":
                        for i, parts in enumerate((wg_s, wu_s)):
                            ins = project(two[:, i, :], tile_of(parts, slice(c * P, (c + 1) * P)),
                                          tile_of(NT_s, whole), KD)
                    elif kind[:4] == "DOWN":
                        half = KH // 2
                        pe.wait_ge(h_low.sem, h_low.at(rb, half * (c + 1)))
                        for t in range(T):
                            ins = project(two[:, t, :], tile_of(H_s, slice(t * P, (t + 1) * P)),
                                          lambda k: [w[:, half * c + k, :] for w in wd_s], half)
                    ins.then_inc(gen_full, 1)

                def scores(i):
                    q = QT[:, i // 2 % 2, i % 2, :]
                    if i >= NP // 2:
                        for bank, value in ph.read(f"aQ{i // 2}"):
                            pe.wait_ge(gen_read[bank], value)
                    for t in range(T):
                        keys = P * (t + 1)
                        pe.wait_ge(s_masked.sem, s_masked.at(b, 2 * i + t - 1))
                        pe.matmul(s_ps[t][:, 0:2 * keys], q[:, t * P:(t + 1) * P], KB[:, i // 2, :, 0:keys],
                                  start=True, stop=True).then_inc(s_full.sem, 1)

                def probs_transposed(i):
                    pe.wait_ge(p_ready.sem, p_ready.at(b, i + 1))
                    sm = SM[:, i % 2, :]
                    pe.wait_ge(pt0_ready.sem, pt0_ready.at(b, i))
                    for h in range(2):
                        pe.transpose(pt_ps[0][:, h * S:h * S + P], sm[:, h * P:(h + 1) * P], ident[:, :])
                        ins = pe.transpose(pt_ps[0][:, h * S + P:(h + 1) * S],
                                           sm[:, 2 * P + h * S:2 * P + h * S + P], ident[:, :])
                    ins.then_inc(pt_full.sem, 1)
                    pe.wait_ge(pt1_ready.sem, pt1_ready.at(b, i))
                    for h in range(2):
                        ins = pe.transpose(pt_ps[1][:, h * P:(h + 1) * P],
                                           sm[:, 2 * P + h * S + P:2 * P + (h + 1) * S], ident[:, :])
                    ins.then_inc(pt_full.sem, 1)

                def values(i):
                    pe.wait_ge(pt0_ready.sem, pt0_ready.at(b, i + 1))
                    pe.wait_ge(pt1_ready.sem, pt1_ready.at(b, i + 1))
                    pe.wait_ge(z_low.sem, z_low.at(b, i // 2))
                    at = i % 2 * S
                    pt = PT[:, i % 2, :]
                    for h in range(2):
                        v = slice((i // 2 * 2 + h) * E, (i // 2 * 2 + h + 1) * E)
                        rows = slice(h * E, (h + 1) * E)
                        pe.matmul(z_ps[rows, at:at + S], Vt[:, 0, v], pt[:, h * S:(h + 1) * S],
                                  start=True, stop=False)
                        ins = pe.matmul(z_ps[rows, at + P:at + S], Vt[:, 1, v],
                                        pt[:, 2 * S + h * P:2 * S + (h + 1) * P], start=False, stop=True)
                    ins.then_inc(z_full.sem, 1)

                if ph.attn and not ph.rest:
                    for bank in range(BANKS):
                        pe.wait_ge(gen_read[bank], ph.turn)
                for i in range(len(SEQUENCE)):
                    for name, pair in ph.step(i):
                        if name == "S":
                            scores(pair)
                        elif name == "T":
                            probs_transposed(pair)
                        elif name == "P":
                            values(pair)
                        else:
                            if name == "nQ0":
                                pe.wait_ge(xT_high.sem, xT_high.at(b + 1, 1))
                                pe.wait_ge(xT_low.sem, xT_low.at(b + 1, 1))
                            if not ph.attn and ph.next:
                                pe.wait_ge(w_low.sem, {"Q": 2, "K": 3, "V": 4}[name[1]])
                            if not ph.rest and name == "aOUT":
                                pe.wait_ge(w_low.sem, len(weights))
                                pe.wait_ge(small_in.sem, 16 * 4)
                                pe.wait_ge(pool_set.sem, SETS + 1)
                            fill(name)

            pe.wait_ge(pool_set.sem, pool_set.at(0, SETS))
            phases(pe, body)

        @block.scalar
        def _(act):
            def copy(o, i):
                return act.activation(o, i, ACT.Copy)

            def split_weight(n):
                act.wait_ge(staged[n % 2].sem, staged[n % 2].at(0, n // 2 + 1))
                copy(weights[n][1][0], stage_of(n)).then_inc(w_high.sem, 1)

            def body(ph):
                b, rb = ph.b, ph.rb

                def gated_high(m):
                    for bank, value in ph.read(f"rFFN{m}"):
                        act.wait_ge(gen_read[bank], value)
                    if m == KH // 2:
                        act.wait_ge(gen_full, ph.full("rDOWN0"))
                    copy(H_s[0][:, m % (KH // 2), :], G[:, m % 2, :]).then_inc(h_high.sem, 1)

                def fill(name):
                    ps = gen[ph.bank(name)]
                    read_out = gen_read[ph.bank(name)]
                    kind, c = name[1:], int(name[-1]) if name[-1].isdigit() else 0
                    if kind[:4] == "DOWN":
                        gated_high(KH // 2 * (c + 1) - 1)
                    if kind[0] == "V" or kind in ("OUT", "XV", "XOUT") or kind[:3] == "SIM" or kind[:4] == "DOWN":
                        return
                    act.wait_ge(gen_full, ph.full(name))
                    if kind[0] == "Q":
                        copy(QT[:, c % 2, :, :], halves_view(ps[:, :])).then_inc(read_out, 1)
                    elif kind[0] == "K":
                        for h in range(2):
                            rows = slice(h * E, (h + 1) * E)
                            ins = copy(KB[rows, 2 * c:2 * c + 2, h, :], halves_view(ps[rows, :]))
                        ins.then_inc(read_out, 1)
                    elif kind[:2] == "T1":
                        act.wait_ge(gen_full, ph.full("rT11"))
                        act.activation(XN[:, c * S:(c + 1) * S], ps[:, 0:S], ACT.Identity, scale=lnw[:, c:c + 1],
                                       bias=lnb[:, c:c + 1]).then_inc(read_out, 1)
                        if c == 1:
                            for bank, value in ph.read("rT10", "rT11"):
                                act.wait_ge(gen_read[bank], value)
                            copy(NT_s[0][:, :, :], halves_view(XN[:, :])).then_inc(nt_high.sem, 1)
                    elif kind == "XK":
                        for h in range(2):
                            rows = slice(h * E, (h + 1) * E)
                            ins = copy(KX[rows, :, h * V:(h + 1) * V],
                                       ps[rows, :].rearrange("p (m v) -> p m v", m=XP)[:, :, 0:V])
                        ins.then_inc(read_out, 1)
                    elif kind[:2] == "XQ":
                        copy(QX_q[:, 2 * c:2 * c + 2, :], halves_view(ps[:, :])).then_inc(read_out, 1)
                    elif kind[:2] == "T2":
                        copy(QX_p[:, 4 * c:4 * c + 4, :], ps[:, :].rearrange("p (h s) -> p h s", h=4))\
                            .then_inc(read_out, 1)
                    elif kind[:3] == "XPV":
                        copy(ZX_s[0][:, :, c * P:(c + 1) * P], ps[:, :].rearrange("p (m s) -> p m s", m=XP))\
                            .then_inc(zx_high.sem, 1)
                    elif kind[:2] == "T3":
                        copy(NT_s[0][:, c, :], ps[:, 0:S]).then_inc(nt_high.sem, 1)
                    elif kind[:3] == "FFN":
                        if c >= 2:
                            act.wait_ge(h_low.sem, h_low.at(rb, c - 1))
                        act.activation(G[:, c % 2, :], ps[:, 0:S], ACT.Tanh, scale=0.5 * QUANT)\
                            .then_inc(tanh_done.sem, 1)
                        if c % (KH // 2) > 0:
                            gated_high(c - 1)

                def exps(i):
                    act.wait_ge(s_masked.sem, s_masked.at(b, 2 * i + 2))
                    sm = SM[:, i % 2, :]
                    for n, (at, keys) in enumerate(((0, P), (P, P), (2 * P, S), (2 * P + S, S))):
                        part = sm[:, at:at + keys]
                        ins = act.activation(part, part, ACT.Exp, scale=-1.0, bias=least[:, i % 2, n:n + 1],
                                             accum_out=total[:, i % 2, n:n + 1])
                    ins.then_inc(exp_done.sem, 1)

                def context_exps(t):
                    act.wait_ge(sx_shifted.sem, sx_shifted.at(rb, t + 1))
                    act.activation(SX[:, :, :], SX[:, :, :], ACT.Exp)
                    act.activation(pmax[:, 2, :], pmax[:, 1, :], ACT.Exp).then_inc(sx_exp.sem, 1)

                def split_x():
                    act.wait_ge(xT_loaded.sem, xT_loaded.at(b + 1, 1))
                    copy(xT_s[0][:, :, :], xT_in[:, :, :]).then_inc(xT_high.sem, 1)

                if ph.next and not ph.attn:
                    split_x()
                if ph.rest:
                    act.wait_ge(ctx_loaded.sem, ctx_loaded.at(rb, 1))
                    copy(ctx_s[0][:, :, :], ctx_in[:, :, :]).then_inc(ctx_high.sem, 1)
                for i in range(len(SEQUENCE)):
                    for name, pair in ph.step(i):
                        if name == "T":
                            act.wait_ge(pt_full.sem, pt_full.at(b, 2 * pair + 1))
                            act.wait_ge(z_full.sem, z_full.at(b, pair - 1))
                            copy(PT[:, pair % 2, 0:2 * S], pt_ps[0][:, :]).then_inc(pt0_ready.sem, 1)
                        elif name == "S":
                            exps(pair)
                        elif name == "P":
                            if pair % 2:
                                act.wait_ge(z_full.sem, z_full.at(b, pair + 1))
                                copy(Z_s[0][:, pair - 1:pair + 1, :], halves_view(z_ps[:, :])).then_inc(z_high.sem, 1)
                        else:
                            fill(name)
                            if name in ("rSIM01", "rSIM11"):
                                context_exps(int(name[4]))
                    if ph.next and ph.attn and i == 5:
                        split_x()
                    if ph.attn and not ph.rest:
                        for n in late_weights[i]:
                            split_weight(n)

            for n in range(EARLY):
                split_weight(n)
            act.wait_ge(pool_set.sem, pool_set.at(0, SETS))
            act.wait_ge(small_in.sem, small_in.at(0, 4))
            phases(act, body)

        @block.vector
        def _(dve):
            def split_weight(n):
                dve.wait_ge(w_high.sem, w_high.at(0, n + 1))
                high, low = weights[n][1]
                dve.tensor_tensor(low, stage_of(n), high.bitcast(F32), ALU.subtract).then_inc(w_low.sem, 1)

            def stand_alone():
                dve.sem_inc(waited, 1)

            def body(ph):
                b, rb = ph.b, ph.rb
                dve_a.begin()
                dve_r.begin()

                def moments_of(src, k, chain, batch, ready):
                    for t in range(T):
                        ins = dve.bn_stats(stats[:, k, t, :], src[:, t, :])
                    ins.then_inc(chain.next(), 1)
                    dve.wait_ge(chain.sem, chain.so_far(batch))
                    stand_alone()
                    for t in range(T):
                        ins = dve.bn_aggr(moments[:, k, t, :], stats[:, k, t, :])
                    ins.then_inc(ready.sem, 1)

                def normed(dst, src, k):
                    for t in range(T):
                        ins = dve.tensor_scalar(dst[:, t, :], src[:, t, :], moments[:, k, t, 0:1],
                                                rstd[:, k, t:t + 1], ALU.subtract, ALU.mult)
                    return ins

                def masks():
                    dve.wait_ge(mask_loaded.sem, mask_loaded.at(rb, 1))
                    dve.tensor_scalar(allowed[:, :, :], mask_in[:, :, :], 0.0, None, ALU.not_equal).then_inc(dve_r.next(), 1)
                    dve.wait_ge(dve_r.sem, dve_r.so_far(rb))
                    for t in range(T):
                        ins = dve.tensor_tensor_scan(taken[:, t, :], ones[:, 0:V], allowed[:, t, :], 0.0,
                                                     ALU.mult, ALU.add)
                    ins.then_inc(dve_r.next(), 1)
                    dve.wait_ge(dve_r.sem, dve_r.so_far(rb))
                    found = taken[:, :, V - 1]
                    dve.tensor_scalar(count[:, :, 0], found, -1.0, float(TOP), ALU.mult, ALU.add)
                    dve.tensor_scalar(count[:, :, 1], found, float(TOP), NEG, ALU.is_ge, ALU.mult).then_inc(dve_r.next(), 1)
                    dve.wait_ge(dve_r.sem, dve_r.so_far(rb))
                    dve.tensor_scalar(count[:, :, 0], count[:, :, 0], 0.0, None, ALU.max)
                    dve.tensor_scalar(pad_bias[:, :], count[:, :, 1], PAD_BIAS, None, ALU.add)
                    dve.scalar_tensor_tensor(out=taken[:, :, :], in0=taken[:, :, :], scalar=float(TOP),
                                                        in1=allowed[:, :, :], op0=ALU.is_le, op1=ALU.mult).then_inc(dve_r.next(), 1)
                    dve.wait_ge(dve_r.sem, dve_r.so_far(rb))
                    dve.tensor_scalar(taken[:, :, :], taken[:, :, :], -1.0, -NEG, ALU.add, ALU.mult)\
                        .then_inc(mask_read.sem, 1)

                def context_shift(t):
                    for bank, value in ph.read(f"rSIM{t}0", f"rSIM{t}1"):
                        dve.wait_ge(gen_read[bank], value)
                    dve.tensor_reduce(pmax[:, 0, :], SX[:, :, :], AX_X, ALU.max).then_inc(dve_r.next(), 1)
                    dve.wait_ge(dve_r.sem, dve_r.so_far(rb))
                    dve.tensor_scalar(pmax[:, 0, :], pmax[:, 0, :], pad_bias[:, t:t + 1], None, ALU.max).then_inc(dve_r.next(), 1)
                    dve.wait_ge(dve_r.sem, dve_r.so_far(rb))
                    dve.tensor_scalar(pmax[:, 1, :], pmax[:, 0, :], -1.0, pad_bias[:, t:t + 1], ALU.mult, ALU.add)
                    dve.tensor_tensor(SX[:, :, :], SX[:, :, :], pmax[:, 0, :].unsqueeze(2).broadcast_to([P, XH, V]),
                                      ALU.subtract).then_inc(sx_shifted.sem, 1)

                def context_probs(t):
                    dve.wait_ge(sx_exp.sem, sx_exp.at(rb, t + 1))
                    dve.tensor_reduce(den[:, 0, :], SX[:, :, :], AX_X, ALU.add).then_inc(dve_r.next(), 1)
                    dve.wait_ge(dve_r.sem, dve_r.so_far(rb))
                    dve.scalar_tensor_tensor(out=den[:, 1, :], in0=pmax[:, 2, :], scalar=count[:, t, 0:1],
                                                        in1=den[:, 0, :], op0=ALU.mult, op1=ALU.add).then_inc(dve_r.next(), 1)
                    dve.wait_ge(dve_r.sem, dve_r.so_far(rb))
                    dve.reciprocal(den[:, 0, :], den[:, 1, :]).then_inc(dve_r.next(), 1)
                    dve.wait_ge(dve_r.sem, dve_r.so_far(rb))
                    if t > 0:
                        dve.wait_ge(gen_full, ph.full(f"rT2{t - 1}1"))
                    dve.tensor_tensor(PX[:, :, 0:V], SX[:, :, :], den[:, 0, :].unsqueeze(2).broadcast_to([P, XH, V]),
                                      ALU.mult).then_inc(px_ready.sem, 1)

                def fill(name):
                    ps = gen[ph.bank(name)]
                    two = halves_view(ps[:, :])
                    read_out = gen_read[ph.bank(name)]
                    kind, c = name[1:], int(name[-1]) if name[-1].isdigit() else 0
                    if kind[0] == "V":
                        dve.wait_ge(gen_full, ph.full(name))
                        dve.tensor_copy(Vt[:, c, :], ps[:, :]).then_inc(read_out, 1)
                    elif kind == "OUT":
                        dve.wait_ge(x_biased.sem, x_biased.at(b, 1))
                        dve.wait_ge(gen_full, ph.full(name))
                        dve.tensor_tensor(X[:, :, :], two, x_in[:, :, :], ALU.add).then_inc(read_out, 1)
                    elif kind == "T11":
                        dve.wait_ge(nt_high.sem, nt_high.at(rb, 1))
                        dve.tensor_tensor(NT_s[1][:, :, :], halves_view(XN[:, :]), NT_s[0][:, :, :].bitcast(F32),
                                          ALU.subtract).then_inc(nt_low.sem, 1)
                    elif kind == "XV":
                        dve.wait_ge(gen_full, ph.full(name))
                        dve.tensor_copy(VX[:, :], ps[:, :]).then_inc(read_out, 1)
                    elif kind[:3] == "SIM":
                        t = int(kind[3])
                        if name == "rSIM00":
                            dve.wait_ge(mask_read.sem, mask_read.at(rb, 1))
                        if t > 0:
                            dve.wait_ge(px_ready.sem, px_ready.at(rb, t))
                        dve.wait_ge(gen_full, ph.full(name))
                        dve.scalar_tensor_tensor(out=SX[:, 4 * c:4 * c + 4, :],
                                                 in0=ps[:, 0:4 * V].rearrange("p (h v) -> p h v", h=4), scalar=SCALE,
                                                 in1=taken[:, t, :].unsqueeze(1).broadcast_to([P, 4, V]),
                                                 op0=ALU.mult, op1=ALU.add).then_inc(read_out, 1)
                    elif kind[:3] == "XPV":
                        dve.wait_ge(zx_high.sem, zx_high.at(rb, c + 1))
                        cols = slice(c * P, (c + 1) * P)
                        dve.tensor_tensor(ZX_s[1][:, :, cols], ps[:, :].rearrange("p (m s) -> p m s", m=XP),
                                          ZX_s[0][:, :, cols].bitcast(F32), ALU.subtract).then_inc(read_out, 1)
                    elif kind == "XOUT":
                        dve.wait_ge(gen_full, ph.full(name))
                        dve.tensor_tensor(X[:, :, :], two, X[:, :, :], ALU.add).then_inc(read_out, 1)
                        for bank, value in ph.read(name):
                            dve.wait_ge(gen_read[bank], value)
                        moments_of(X, 2, dve_r, rb, moments_r)
                        dve.wait_ge(rstd_r.sem, rstd_r.at(rb, 1))
                        normed(X, X, 2).then_inc(x2_ready.sem, 1)
                    elif kind[:2] == "T3":
                        dve.wait_ge(nt_high.sem, nt_high.at(rb, 2 + c))
                        dve.tensor_tensor(NT_s[1][:, c, :], ps[:, 0:S], NT_s[0][:, c, :].bitcast(F32),
                                          ALU.subtract).then_inc(read_out, 1)
                    elif kind[:3] == "FFN":
                        dve.wait_ge(tanh_done.sem, tanh_done.at(rb, c + 1))
                        g = G[:, c % 2, :]
                        dve.scalar_tensor_tensor(out=g, in0=g, scalar=1.0, in1=ps[:, 0:S],
                                                            op0=ALU.add, op1=ALU.mult).then_inc(dve_r.next(), 1)
                        dve.wait_ge(dve_r.sem, dve_r.so_far(rb))
                        dve.tensor_tensor(g, ps[:, S:2 * S], g, ALU.mult).then_inc(read_out, 1)
                    elif kind == "DOWN0":
                        dve.wait_ge(y_free.sem, y_free.at(rb, 1))
                        dve.wait_ge(gen_full, ph.full(name))
                        dve.scalar_tensor_tensor(out=Y[:, :, :], in0=two, scalar=0.5 * QUANT ** 3, in1=X[:, :, :],
                                                 op0=ALU.mult, op1=ALU.add).then_inc(read_out, 1)
                    elif kind == "DOWN1":
                        dve.wait_ge(gen_full, ph.full(name))
                        dve.scalar_tensor_tensor(out=Y[:, :, :], in0=two, scalar=0.5 * QUANT ** 3, in1=Y[:, :, :],
                                                 op0=ALU.mult, op1=ALU.add).then_inc(read_out, 1)

                def masked(i):
                    dve.wait_ge(pt_full.sem, pt_full.at(b, 2 * i - 2))
                    for t in range(T):
                        keys = P * (t + 1)
                        dve.wait_ge(s_full.sem, s_full.at(b, 2 * i + t + 1))
                        stand_alone()
                        for h in range(2):
                            at = 2 * P * t + h * keys
                            ins = dve.tensor_tensor_reduce(SM[:, i % 2, at:at + keys],
                                                           s_ps[t][:, h * keys:(h + 1) * keys],
                                                           causal[:, S - keys:S], -SCALE, -3 * NEG, ALU.add, ALU.min,
                                                           least[:, i % 2, 2 * t + h:2 * t + h + 1])
                        ins.then_inc(s_masked.sem, 1)

                def first_normed():
                    dve.wait_ge(rstd_a.sem, rstd_a.at(b, 1))
                    normed(X, X, 0).then_inc(dve_a.next(), 1)
                    dve.wait_ge(dve_a.sem, dve_a.so_far(b))
                    moments_of(X, 1, dve_a, b, moments_a)

                def normalised(i):
                    dve.wait_ge(exp_done.sem, exp_done.at(b, i + 1))
                    dve.reciprocal(total[:, i % 2, :], total[:, i % 2, :]).then_inc(dve_a.next(), 1)
                    dve.wait_ge(dve_a.sem, dve_a.so_far(b))
                    for n, (at, keys) in enumerate(((0, P), (P, P), (2 * P, S), (2 * P + S, S))):
                        part = SM[:, i % 2, at:at + keys]
                        ins = dve.tensor_scalar(part, part, total[:, i % 2, n:n + 1], None, ALU.mult)
                    ins.then_inc(p_ready.sem, 1)

                for i in range(len(SEQUENCE)):
                    if ph.attn and 1 <= i <= NP:
                        normalised(i - 1)
                    for name, pair in ph.step(i):
                        if name == "T":
                            dve.wait_ge(pt_full.sem, pt_full.at(b, 2 * pair + 2))
                            dve.wait_ge(z_full.sem, z_full.at(b, pair - 1))
                            dve.tensor_copy(PT[:, pair % 2, 2 * S:PAIR], pt_ps[1][:, 0:2 * P])\
                                .then_inc(pt1_ready.sem, 1)
                        elif name == "S":
                            masked(pair)
                        elif name == "P":
                            if pair % 2:
                                dve.wait_ge(z_high.sem, z_high.at(b, (pair + 1) // 2))
                                dve.tensor_tensor(Z_s[1][:, pair - 1:pair + 1, :], halves_view(z_ps[:, :]),
                                                  Z_s[0][:, pair - 1:pair + 1, :].bitcast(F32),
                                                  ALU.subtract).then_inc(z_low.sem, 1)
                        else:
                            if name == "rT10":
                                dve.wait_ge(rstd_a.sem, rstd_a.at(rb, 2))
                                normed(XN_t, X, 1).then_inc(xn_ready.sem, 1)
                            if name == "rSIM10":
                                context_probs(0)
                            if name == "rDOWN1" and ph.attn:
                                first_normed()
                            fill(name)
                            if name in ("rSIM01", "rSIM11"):
                                context_shift(int(name[4]))
                            if name == "aOUT":
                                for bank, value in ph.read(name):
                                    dve.wait_ge(gen_read[bank], value)
                                moments_of(X, 0, dve_a, b, moments_a)
                    if ph.rest and i == 2:
                        masks()
                    if ph.rest and i == 5:
                        context_probs(1)
                    if ph.attn and not ph.rest:
                        for n in late_weights[i]:
                            split_weight(n)
                if ph.attn and not ph.rest:
                    first_normed()
                if ph.attn:
                    dve_a.end()
                if ph.rest:
                    for bank, value in ph.read("rDOWN1"):
                        dve.wait_ge(gen_read[bank], value)
                    moments_of(Y, 3, dve_r, rb, moments_r)
                if ph.rest:
                    dve.wait_ge(rstd_r.sem, rstd_r.at(rb, 2))
                    normed(Y, Y, 3).then_inc(out_ready.sem, 1)
                    dve_r.end()
                if ph.attn and not ph.rest:
                    dve.wait_ge(pool_set.sem, SETS + 1)

            for n in range(EARLY):
                split_weight(n)
            dve.wait_ge(pool_set.sem, pool_set.at(0, SETS))
            phases(dve, body)

        @block.gpsimd
        def _(pool):
            def body(ph):
                b, rb = ph.b, ph.rb
                pool_a.begin()
                pool_r.begin()

                def inverse_deviation(k, chain, batch, moments_ready, rstd_ready, count):
                    pool.wait_ge(moments_ready.sem, moments_ready.at(batch, count))
                    pool.tensor_tensor(var[:, k, :], moments[:, k, :, 1], eps[:, :], ALU.add)\
                        .then_inc(chain.next(), 1)
                    pool.wait_ge(chain.sem, chain.so_far(batch))
                    pool.tensor_tensor(rstd[:, k, :], var[:, k, :], minus_half[:, :], ALU.pow)\
                        .then_inc(rstd_ready.sem, 1)

                if ph.rest:
                    pool.wait_ge(ctx_high.sem, ctx_high.at(rb, 1))
                    pool.tensor_tensor(ctx_s[1][:, :, :], ctx_in[:, :, :], ctx_s[0][:, :, :].bitcast(F32),
                                       ALU.subtract).then_inc(ctx_low.sem, 1)
                if ph.next:
                    pool.wait_ge(xT_high.sem, xT_high.at(b + 1, 1))
                    pool.tensor_tensor(xT_s[1][:, :, :], xT_in[:, :, :], xT_s[0][:, :, :].bitcast(F32),
                                       ALU.subtract).then_inc(xT_low.sem, 1)
                if ph.attn:
                    pool.wait_ge(x_loaded.sem, x_loaded.at(b, 1))
                    pool.tensor_tensor(x_in[:, :, :], x_in[:, :, :], bias[:, :].unsqueeze(1).broadcast_to([P, T, D]),
                                       ALU.add).then_inc(x_biased.sem, 1)
                if ph.attn and not ph.rest:
                    pool.wait_ge(w_low.sem, len(weights))
                    pool.memset(PX[:, :, :], 0.0).then_inc(pool_set.sem, 1)
                if ph.rest:
                    inverse_deviation(2, pool_r, rb, moments_r, rstd_r, 1)
                    for m in range(KH):
                        pool.wait_ge(h_high.sem, h_high.at(rb, m + 1))
                        slot = m % (KH // 2)
                        pool.tensor_tensor(H_s[1][:, slot, :], G[:, m % 2, :], H_s[0][:, slot, :].bitcast(F32),
                                           ALU.subtract).then_inc(h_low.sem, 1)
                if ph.attn:
                    inverse_deviation(0, pool_a, b, moments_a, rstd_a, 1)
                    inverse_deviation(1, pool_a, b, moments_a, rstd_a, 2)
                if ph.rest:
                    inverse_deviation(3, pool_r, rb, moments_r, rstd_r, 2)

            pool.memset(Y[:, :, :], 0.0).then_inc(y_free.sem, 16)
            zeros = [ident, ctx_in, KB, causal, KX]
            for z in zeros:
                pool.memset(z[tuple([slice(None)] * len(z.shape))], 0.0).then_inc(pool_set.sem, 1)
            pool.memset(ones[:, :], 1.0).then_inc(pool_set.sem, 1)
            pool.memset(minus_half[:, :], -0.5).then_inc(pool_set.sem, 1)
            pool.memset(eps[:, :], EPS).then_inc(pool_set.sem, 1)
            pool.wait_ge(pool_set.sem, pool_set.at(0, 8))
            pool.affine_select(out=ident[:, :], in_=ident[:, :], compare_op=ALU.not_equal, fill=1.0, base=0,
                               pattern=[[-1, P]], channel_multiplier=1).then_inc(pool_set.sem, 1)
            pool.affine_select(out=causal[:, P:S], in_=causal[:, P:S], compare_op=ALU.is_ge, fill=NEG, base=0,
                               pattern=[[-1, P]], channel_multiplier=1).then_inc(pool_set.sem, 1)
            pool.wait_ge(small_in.sem, small_in.at(0, 4))
            phases(pool, body)


_ORDER = ["x", "xT", "ctxT", "maskT", "wq", "wk", "wv", "wo", "b_out", "ln_w", "ln_b", "xwq", "xwkv", "xwo",
          "wg", "wu", "wd"]


def kernel(x, ctx_1024, mask_BxS2xS_ik0, L0_attn_W_Q, L0_attn_W_K, L0_attn_W_V, L0_attn_W_out, L0_attn_b_out,
           L0_xattn_ln_w, L0_xattn_ln_b, L0_xattn_Wq, L0_xattn_Wkv, L0_xattn_Wout, L0_ffn_w_gate, L0_ffn_w_up,
           L0_ffn_w_down):
    import numpy as np
    import concourse.bacc as bacc
    from concourse.bass_utils import run_bass_kernel_spmd

    def lay(a, *axes):
        return np.ascontiguousarray(np.transpose(np.asarray(a), axes))

    D, NH, E = L0_attn_W_Q.shape
    pairs = (NH // 4, 2, 2)
    wq = lay(np.asarray(L0_attn_W_Q).reshape(D, *pairs, E), 0, 1, 3, 2, 4).reshape(D, NH * E)
    wo = lay(np.asarray(L0_attn_W_out).reshape(E, *pairs, D), 1, 3, 2, 0, 4).reshape(NH * E, D)
    arrays = {
        "x": lay(x, 0, 1, 2), "xT": lay(x, 0, 2, 1), "ctxT": lay(ctx_1024, 0, 2, 1),
        "maskT": lay(mask_BxS2xS_ik0, 0, 2, 1),
        "wq": wq, "wk": lay(L0_attn_W_K, 0, 1, 2).reshape(D, -1), "wv": lay(L0_attn_W_V, 0, 1, 2).reshape(D, -1),
        "wo": wo, "b_out": lay(L0_attn_b_out, 0), "ln_w": lay(np.asarray(L0_xattn_ln_w).reshape(-1, P), 1, 0),
        "ln_b": lay(np.asarray(L0_xattn_ln_b).reshape(-1, P), 1, 0),
        "xwq": lay(L0_xattn_Wq, 0, 1), "xwkv": lay(L0_xattn_Wkv, 0, 1), "xwo": lay(L0_xattn_Wout, 0, 1),
        "wg": lay(L0_ffn_w_gate, 1, 0), "wu": lay(L0_ffn_w_up, 1, 0), "wd": lay(L0_ffn_w_down, 1, 0),
    }
    nc = bacc.Bacc("TRN2", target_bir_lowering=False, num_devices=1)
    inputs = {f"in_{n}": arrays[n] for n in _ORDER}
    args = [nc.dram_tensor(n, a.shape, mybir.dt.from_np(a.dtype), kind="ExternalInput").ap()
            for n, a in inputs.items()]
    out = nc.dram_tensor("out", x.shape, F32, kind="ExternalOutput").ap()
    decoder_layer(nc, *args, out)
    r = run_bass_kernel_spmd(nc, [inputs], core_ids=[0])
    return r.results[0]["out"]
```
